# Optimizing a Trainium2 kernel written in Bass

```python
import numpy as np
import jax
import jax.numpy as jnp

def _softmax(x, axis=-1):
    return jax.nn.softmax(x, axis=axis)

def _gelu(x):
    return jax.nn.gelu(x, approximate=True)

def _silu(x):
    return jax.nn.silu(x)

def _sigmoid(x):
    return jax.nn.sigmoid(x)

def _layernorm(x, axis=-1, eps=1e-05):
    m = jnp.mean(x, axis=axis, keepdims=True)
    v = jnp.var(x, axis=axis, keepdims=True)
    return (x - m) / jnp.sqrt(v + eps)

def _scatter_add(tgt, idx, src, axis=0):
    return tgt.at[idx].add(src)

def _segment_sum(src, seg, n):
    return jax.ops.segment_sum(src, seg, n)
kernel_name = 'mk_seq_postln_d2_jaxref_r8_8e4852'

def setup_inputs(seed: int=0):
    np.random.seed(seed)
    _w = jnp.asarray

    def _L0_attn_setup():
        import jax, jax.numpy as jnp
        import numpy as np
        EPS = 1e-06

        def _rms(x):
            return x * jax.lax.rsqrt(jnp.mean(x * x, axis=-1, keepdims=True) + EPS)
        key = jax.random.key(seed)
        ks = jax.random.split(key, 10)
        B, S, D, MULT = (4, 512, 128, 4)
        H = MULT * D

        def w(k, shape, s=0.02):
            return jax.random.normal(k, shape, jnp.float32) * s
        return {'x': jax.random.normal(ks[0], (B, S, D), jnp.float32), 'Wk': w(ks[1], (D, D)), 'Wv': w(ks[2], (D, D)), 'Wr': w(ks[3], (D, D)), 'Wo': w(ks[4], (D, D)), 'time_decay': jax.random.normal(ks[5], (D,), jnp.float32) * 0.01 - 5.0, 'time_first': jax.random.normal(ks[6], (D,), jnp.float32) * 0.01, 'mixer_scale': jnp.ones((D,), jnp.float32), 'Wfc': w(ks[7], (H, D)), 'Wmlp': w(ks[8], (D, H)), 'mlp_scale': jnp.ones((D,), jnp.float32)}
    _L0_attn_in = _L0_attn_setup()

    def _L0_ffn_setup():
        import jax, jax.numpy as jnp
        import numpy as np
        E = 8
        D = 128
        H = 256
        TOP_K = 2
        key = jax.random.key(seed)
        k_x, k_g, k_w1, k_w2 = jax.random.split(key, 4)
        B, S = (4, 256)
        inp = {'input': jax.random.normal(k_x, (B, S, D), dtype=jnp.float32), 'Wg': jax.random.normal(k_g, (D, E), dtype=jnp.float32) * 0.02, 'W1': jax.random.normal(k_w1, (E, D, H), dtype=jnp.float32) * 0.02, 'b1': jnp.zeros((E, H), dtype=jnp.float32), 'W2': jax.random.normal(k_w2, (E, H, D), dtype=jnp.float32) * 0.02, 'b2': jnp.zeros((E, D), dtype=jnp.float32)}
        return inp
    _L0_ffn_in = _L0_ffn_setup()

    def _L1_attn_setup():
        import jax, jax.numpy as jnp
        import numpy as np
        EPS = 1e-06

        def _rmsnorm(x, w):
            dt = x.dtype
            xf = x.astype(jnp.float32)
            var = jnp.mean(xf * xf, axis=-1, keepdims=True)
            xf = xf * jax.lax.rsqrt(var + EPS)
            return xf.astype(dt) * w
        key = jax.random.key(seed)
        ks = jax.random.split(key, 4)
        B, N, C = (4, 256, 128)
        H = 16
        D = C // H
        x = jax.random.normal(ks[0], (B, N, C), dtype=jnp.float32)
        W_qkv = jax.random.normal(ks[1], (C, 3 * C), dtype=jnp.float32) * (1.0 / np.sqrt(C))
        b_qkv = jnp.zeros((3 * C,), dtype=jnp.float32)
        W_proj = jax.random.normal(ks[2], (C, C), dtype=jnp.float32) * (1.0 / np.sqrt(C))
        b_proj = jnp.zeros((C,), dtype=jnp.float32)
        qn_w = jnp.ones((D,), dtype=jnp.float32)
        kn_w = jnp.ones((D,), dtype=jnp.float32)
        return {'x': x, 'W_qkv': W_qkv, 'b_qkv': b_qkv, 'W_proj': W_proj, 'b_proj': b_proj, 'qn_w': qn_w, 'kn_w': kn_w}
    _L1_attn_in = _L1_attn_setup()

    def _L1_ffn_setup():
        import jax, jax.numpy as jnp
        import numpy as np
        B, S, D, H, E = (4, 256, 128, 16, 4)
        key = jax.random.key(seed)
        ks = jax.random.split(key, 8)
        w = lambda k, shape: jax.random.normal(k, shape, jnp.float32) * 0.02
        return {'x': jax.random.normal(ks[0], (B, S, D), jnp.float32), 'router_w': w(ks[1], (D, E)), 'router_b': jnp.zeros((E,), jnp.float32), 'wq': w(ks[2], (E, D, D)), 'bq': jnp.zeros((E, D), jnp.float32), 'wk': w(ks[3], (E, D, D)), 'bk': jnp.zeros((E, D), jnp.float32), 'wv': w(ks[4], (E, D, D)), 'bv': jnp.zeros((E, D), jnp.float32), 'wo': w(ks[5], (E, D, D)), 'bo': jnp.zeros((E, D), jnp.float32)}
    _L1_ffn_in = _L1_ffn_setup()
    _d = {'L0_attn_x': _L0_attn_in['x'], 'L0_attn_Wk': _L0_attn_in['Wk'], 'L0_attn_Wv': _L0_attn_in['Wv'], 'L0_attn_Wr': _L0_attn_in['Wr'], 'L0_attn_Wo': _L0_attn_in['Wo'], 'L0_attn_time_decay': _L0_attn_in['time_decay'], 'L0_attn_time_first': _L0_attn_in['time_first'], 'L0_attn_mixer_scale': _L0_attn_in['mixer_scale'], 'L0_attn_Wfc': _L0_attn_in['Wfc'], 'L0_attn_Wmlp': _L0_attn_in['Wmlp'], 'L0_attn_mlp_scale': _L0_attn_in['mlp_scale'], 'L0_ffn_Wg': _L0_ffn_in['Wg'], 'L0_ffn_W1': _L0_ffn_in['W1'], 'L0_ffn_b1': _L0_ffn_in['b1'], 'L0_ffn_W2': _L0_ffn_in['W2'], 'L0_ffn_b2': _L0_ffn_in['b2'], 'L1_attn_W_qkv': _L1_attn_in['W_qkv'], 'L1_attn_b_qkv': _L1_attn_in['b_qkv'], 'L1_attn_W_proj': _L1_attn_in['W_proj'], 'L1_attn_b_proj': _L1_attn_in['b_proj'], 'L1_attn_qn_w': _L1_attn_in['qn_w'], 'L1_attn_kn_w': _L1_attn_in['kn_w'], 'L1_ffn_router_w': _L1_ffn_in['router_w'], 'L1_ffn_router_b': _L1_ffn_in['router_b'], 'L1_ffn_wq': _L1_ffn_in['wq'], 'L1_ffn_bq': _L1_ffn_in['bq'], 'L1_ffn_wk': _L1_ffn_in['wk'], 'L1_ffn_bk': _L1_ffn_in['bk'], 'L1_ffn_wv': _L1_ffn_in['wv'], 'L1_ffn_bv': _L1_ffn_in['bv'], 'L1_ffn_wo': _L1_ffn_in['wo'], 'L1_ffn_bo': _L1_ffn_in['bo']}
    _x0 = _d['L0_attn_x']
    _d['L0_attn_x'] = jax.random.normal(jax.random.fold_in(jax.random.key(seed), 1), (16, 256, 128), dtype=_x0.dtype)
    del _x0
    return _d

def reference(L0_attn_x, L0_attn_Wk, L0_attn_Wv, L0_attn_Wr, L0_attn_Wo, L0_attn_time_decay, L0_attn_time_first, L0_attn_mixer_scale, L0_attn_Wfc, L0_attn_Wmlp, L0_attn_mlp_scale, L0_ffn_Wg, L0_ffn_W1, L0_ffn_b1, L0_ffn_W2, L0_ffn_b2, L1_attn_W_qkv, L1_attn_b_qkv, L1_attn_W_proj, L1_attn_b_proj, L1_attn_qn_w, L1_attn_kn_w, L1_ffn_router_w, L1_ffn_router_b, L1_ffn_wq, L1_ffn_bq, L1_ffn_wk, L1_ffn_bk, L1_ffn_wv, L1_ffn_bv, L1_ffn_wo, L1_ffn_bo):

    def _L0_attn_ref(x, Wk, Wv, Wr, Wo, time_decay, time_first, mixer_scale, Wfc, Wmlp, mlp_scale):
        import jax, jax.numpy as jnp
        import numpy as np
        EPS = 1e-06

        def _rms(x):
            return x * jax.lax.rsqrt(jnp.mean(x * x, axis=-1, keepdims=True) + EPS)
        normed = _rms(x)
        k = normed @ Wk.T
        v = normed @ Wv.T
        r = jax.nn.sigmoid(normed @ Wr.T)
        ew = jnp.exp(-jnp.exp(time_decay))
        eu = jnp.exp(time_first)
        kv = (k * v).transpose(1, 0, 2)
        state0 = jnp.zeros((x.shape[0], x.shape[2]), x.dtype)

        def step(state, kvt):
            wkv = state + eu * kvt
            return (ew * state + kvt, wkv)
        _, wkv = jax.lax.scan(step, state0, kv)
        mixer_out = r * wkv.transpose(1, 0, 2) @ Wo.T
        x = x + mixer_scale[None, None, :] * mixer_out
        h = jax.nn.leaky_relu(_rms(x) @ Wfc.T, negative_slope=0.5)
        x = x + mlp_scale[None, None, :] * (h * h @ Wmlp.T)
        return x

    def _L0_ffn_ref(input, Wg, W1, b1, W2, b2):
        import jax, jax.numpy as jnp
        import numpy as np
        E = 8
        D = 128
        H = 256
        TOP_K = 2
        logits = jnp.einsum('bsd,de->bse', input, Wg)
        probs = jax.nn.softmax(logits, axis=-1)
        top_vals, top_idx = jax.lax.top_k(probs, TOP_K)
        top_vals = top_vals / jnp.sum(top_vals, axis=-1, keepdims=True)
        onehot = jax.nn.one_hot(top_idx, E, dtype=input.dtype)
        mask = jnp.sum(onehot, axis=2)
        scores = jnp.sum(onehot * top_vals[..., None], axis=2)
        xm = input[None] * jnp.moveaxis(mask, -1, 0)[..., None]
        h = jnp.einsum('ebsd,edh->ebsh', xm, W1) + b1[:, None, None, :]
        h = jax.nn.relu(h)
        y = jnp.einsum('ebsh,ehd->ebsd', h, W2) + b2[:, None, None, :]
        out = jnp.sum(y * jnp.moveaxis(scores, -1, 0)[..., None], axis=0)
        return out

    def _L1_attn_ref(x, W_qkv, b_qkv, W_proj, b_proj, qn_w, kn_w):
        import jax, jax.numpy as jnp
        import numpy as np
        EPS = 1e-06

        def _rmsnorm(x, w):
            dt = x.dtype
            xf = x.astype(jnp.float32)
            var = jnp.mean(xf * xf, axis=-1, keepdims=True)
            xf = xf * jax.lax.rsqrt(var + EPS)
            return xf.astype(dt) * w
        B, N, C = x.shape
        H = 16
        D = C // H
        qkv = jnp.einsum('bnc,cd->bnd', x, W_qkv) + b_qkv
        qkv = qkv.reshape(B, N, 3, H, D)
        q = qkv[:, :, 0].transpose(0, 2, 1, 3)
        k = qkv[:, :, 1].transpose(0, 2, 1, 3)
        v = qkv[:, :, 2].transpose(0, 2, 1, 3)
        q = _rmsnorm(q, qn_w)
        k = _rmsnorm(k, kn_w)
        scale = D ** (-0.5)
        attn = jnp.einsum('bhqd,bhkd->bhqk', q, k) * scale
        attn = jax.nn.softmax(attn, axis=-1)
        out = jnp.einsum('bhqk,bhkd->bhqd', attn, v)
        out = out.transpose(0, 2, 1, 3).reshape(B, N, C)
        out = jnp.einsum('bnc,cd->bnd', out, W_proj) + b_proj
        return out

    def _L1_ffn_ref(x, router_w, router_b, wq, bq, wk, bk, wv, bv, wo, bo):
        import jax, jax.numpy as jnp
        import numpy as np
        B, S, D, H, E = (4, 256, 128, 16, 4)
        b, s, d = x.shape
        e_total = router_w.shape[-1]
        h = H
        hd = d // h
        sm_scale = 0.5
        logits = x @ router_w + router_b
        probs = jax.nn.softmax(logits, axis=-1)
        _, top2 = jax.lax.top_k(probs, 2)
        out = jnp.zeros_like(x)
        bidx = jnp.arange(b)[:, None]
        for e in range(e_total):
            member = (top2 == e).any(-1)
            w_tok = jnp.where(member, probs[..., e], 0.0)
            order = jnp.argsort((~member).astype(jnp.int32), axis=-1, stable=True)
            xg = jnp.take_along_axis(x, order[..., None], axis=1)
            validg = jnp.take_along_axis(member, order, axis=1)
            wg = jnp.take_along_axis(w_tok, order, axis=1)
            q = (xg @ wq[e] + bq[e]).reshape(b, s, h, hd)
            k = (xg @ wk[e] + bk[e]).reshape(b, s, h, hd)
            v = (xg @ wv[e] + bv[e]).reshape(b, s, h, hd)
            att = jnp.einsum('bqhd,bkhd->bhqk', q, k) * sm_scale
            att = jnp.where(validg[:, None, None, :], att, -1000000000.0)
            att = jax.nn.softmax(att, axis=-1)
            y = jnp.einsum('bhqk,bkhd->bqhd', att, v).reshape(b, s, d)
            y = y @ wo[e] + bo[e]
            out = out.at[bidx, order].add(wg[..., None] * y)
        return out
    x = L0_attn_x
    x = _layernorm(x + _L0_attn_ref(x, L0_attn_Wk, L0_attn_Wv, L0_attn_Wr, L0_attn_Wo, L0_attn_time_decay, L0_attn_time_first, L0_attn_mixer_scale, L0_attn_Wfc, L0_attn_Wmlp, L0_attn_mlp_scale), axis=-1)
    x = _layernorm(x + _L0_ffn_ref(x, L0_ffn_Wg, L0_ffn_W1, L0_ffn_b1, L0_ffn_W2, L0_ffn_b2), axis=-1)
    x = _layernorm(x + _L1_attn_ref(x, L1_attn_W_qkv, L1_attn_b_qkv, L1_attn_W_proj, L1_attn_b_proj, L1_attn_qn_w, L1_attn_kn_w), axis=-1)
    x = _layernorm(x + _L1_ffn_ref(x, L1_ffn_router_w, L1_ffn_router_b, L1_ffn_wq, L1_ffn_bq, L1_ffn_wk, L1_ffn_bk, L1_ffn_wv, L1_ffn_bv, L1_ffn_wo, L1_ffn_bo), axis=-1)
    return x

_drawn_inputs = setup_inputs


def setup_inputs(seed=0):
    import zlib

    import numpy as np

    out = dict(_drawn_inputs(seed))
    spreads = {'L0_attn_mixer_scale': (1.0, 0.6),
     'L0_attn_mlp_scale': (1.0, 0.6),
     'L0_ffn_b1': (0.0, 0.492),
     'L0_ffn_b2': (0.0, 0.1),
     'L1_attn_b_qkv': (0.0, 0.1),
     'L1_attn_b_proj': (0.0, 0.1),
     'L1_attn_qn_w': (1.0, 0.572),
     'L1_attn_kn_w': (1.0, 0.6),
     'L1_ffn_router_b': (0.0, 0.369),
     'L1_ffn_bq': (0.0, 0.8),
     'L1_ffn_bk': (0.0, 2.0),
     'L1_ffn_bv': (0.0, 0.8),
     'L1_ffn_bo': (0.0, 0.1)}
    factors = {'L0_attn_Wr': 8.0,
     'L0_attn_time_decay': 8.0,
     'L0_attn_time_first': 64.0,
     'L0_attn_Wfc': 3.686,
     'L0_attn_Wmlp': 3.122,
     'L1_ffn_wq': 8.0,
     'L1_ffn_wk': 8.0,
     'L1_ffn_wv': 8.0,
     'L1_ffn_wo': 5.528}
    for name, (base, spread) in spreads.items():
        noise = np.random.default_rng([zlib.crc32(name.encode()), seed]).standard_normal(out[name].shape)
        drawn = base * np.exp(spread * noise) if base else spread * noise
        out[name] = jnp.asarray(drawn.astype(out[name].dtype))
    for name, factor in factors.items():
        out[name] = (out[name] * factor).astype(out[name].dtype)
    return out
```

```python
import numpy as np
import concourse.bass as bass
from concourse import mybir
from contextlib import ExitStack

F32 = mybir.dt.float32
F16 = mybir.dt.float16
ALU = mybir.AluOpType
ACT = mybir.ActivationFunctionType
AX = mybir.AxisListType.X

B, S, D = 16, 256, 128
P = 128
T = S // P
FC = 4 * D // P
E0, HB = 8, 2
E1 = 4
H, HD = 16, 8
G, J = 4, 4
SLOT = P // J
U = 1 + E1
NORMS = 7
RMS_EPS, LN_EPS = 1e-6, 1e-5
MASKED = -60000.0

SHIFT_ROW, MASK_ROW = 3 * HD, 3 * HD + 1


def program(nc, a, out):
    with ExitStack() as ctx:
        def sb(name, shape, dt=F32):
            return ctx.enter_context(nc.sbuf_tensor(name, shape, dt))

        def sem(name):
            return ctx.enter_context(nc.semaphore(name))

        x_all = sb("x_all", [P, B * T, D])
        y_all = sb("y_all", [P, B * T, D])
        wkvr = sb("wkvr", [D, 3, D])
        wo0 = sb("wo0", [D, D])
        wfc = sb("wfc", [D, FC * P])
        wmlp = sb("wmlp", [P, FC, D])
        wg = sb("wg", [D, E0])
        w1 = sb("w1", [D, E0, HB * P])
        b1 = sb("b1", [P, E0, HB])
        w2 = sb("w2", [P, E0, HB, D])
        b2 = sb("b2", [E0, D])
        wqkv = sb("wqkv", [D, U, 3 * D])
        bqkv = sb("bqkv", [P, U, 3 * D])
        wproj = sb("wproj", [D, U, D])
        bproj = sb("bproj", [P, D])
        bo = sb("bo", [E1, D])
        qk_w = sb("qk_w", [P, 2, HD])
        router_w = sb("router_w", [D, E1])
        router_b = sb("router_b", [P, E1])
        decay = sb("decay", [D, 2])
        mixer_scale = sb("mixer_scale", [P, D])
        mlp_scale = sb("mlp_scale", [P, D])
        ident = sb("ident", [P, P])
        ident16 = sb("ident16", [P, P], F16)
        half = sb("half", [P, 2 * T * 2 * H])
        prio = sb("prio", [P, E0])
        ew = sb("ew", [D, 2])
        ew_bc = sb("ew_bc", [D, S])

        junk = sb("junk", [P, 2, T, D])
        ssq = sb("ssq", [P, 2, T])
        var = sb("var", [P, NORMS - 1, T])
        rstd = sb("rstd", [P, NORMS - 1, T])
        bn6 = sb("bn6", [P, T, 6])
        mv = sb("mv", [P, 4, T, 2])
        xn = sb("xn", [P, T, D])
        xT = sb("xT", [D, S])
        k_sb = sb("k_sb", [D, S])
        er = sb("er", [D, S])
        gate = sb("gate", [D, S])
        kv = sb("kv", [D, S])
        state = sb("state", [D, S + 1])
        mixT = sb("mixT", [D, S])
        tmp = sb("tmp", [P, T, D])
        x1 = sb("x1", [P, T, D])
        z_half = sb("z_half", [P, FC, S])
        h_fc = sb("h_fc", [P, FC, S])
        x3 = sb("x3", [P, T, D])
        x4 = sb("x4", [P, T, D])
        acc = sb("acc", [P, T, D])
        h_moe = sb("h_moe", [P, 2, HB, S])
        lg = sb("lg", [P, T, E0])
        pr = sb("pr", [P, T, E0])
        oh1 = sb("oh1", [P, T, E0])
        oh2 = sb("oh2", [P, T, E0])
        tk = sb("tk", [P, T, E0])
        st1 = sb("st1", [P, 8, T])
        score = sb("score", [P, T, E0])
        scoreT = sb("scoreT", [E0, S])
        member = sb("member", [P, T, E1])
        key_mask = sb("key_mask", [P, T, E1])
        w_tok = sb("w_tok", [P, T, E1])
        qkv = sb("qkv", [P, 3, T, D])
        sq = sb("sq", [P, 2, T, D])
        ms = sb("ms", [P, 2 * T * H])
        rqk = sb("rqk", [P, 2 * T * H])
        q_split = sb("q_split", [P, T, H, SLOT], F16)
        k_split = sb("k_split", [P, T, H, SLOT], F16)
        v_ext = sb("v_ext", [P, T, H, SLOT])
        qT = sb("qT", [P, G, S], F16)
        kT = sb("kT", [P, G, S], F16)
        q_diag = sb("q_diag", [P, J, G, S], F16)
        mx = sb("mx", [P, T, H])
        mneg = sb("mneg", [P, T, H], F16)
        mT = sb("mT", [H, S], F16)
        probs = sb("probs", [P, 2, J, S])
        oT = sb("oT", [P, G, S])
        rden = sb("rden", [P, T, H])
        y_n = sb("y_n", [P, T, D])
        yT = sb("yT", [D, S])

        ps = ctx.enter_context(nc.psum_tensor("ps", [P, 8, 512], F32))
        s_buf = [ps[:, 0:2, :], ps[:, 2:4, :]]
        o_ps = ps[:, 4:6, :].rearrange("p a b -> p (a b)").rearrange("p (g q) -> p g q", g=G)
        m0, m1 = ps[:, 6, :], ps[:, 7, :]
        both = ps[:, 6:8, :]

        loaded = sem("loaded")
        const_ready = sem("const_ready")
        ew_ready = sem("ew_ready")
        exp_decay = sem("exp_decay")
        stored = sem("stored")
        batch_done = sem("batch_done")
        cleared = sem("cleared")
        passed = sem("passed")
        ssq_ready = sem("ssq_ready")
        lnvar_ready = sem("lnvar_ready")
        qkms_ready = sem("qkms_ready")
        rstd_ready = sem("rstd_ready")
        xn_ready = sem("xn_ready")
        xT_ps = sem("xT_ps")
        xT_ready = sem("xT_ready")
        kvr_ps = sem("kvr_ps")
        k_sb_ready = sem("k_sb_ready")
        er_ready = sem("er_ready")
        mixT_ready = sem("mixT_ready")
        mix_ps = sem("mix_ps")
        x1_ready = sem("x1_ready")
        fc_ps = sem("fc_ps")
        zhalf_ready = sem("zhalf_ready")
        hfc_ready = sem("hfc_ready")
        mlp_ps = sem("mlp_ps")
        logit_ps = sem("logit_ps")
        lg_ready = sem("lg_ready")
        pexp_ready = sem("pexp_ready")
        score_ready = sem("score_ready")
        scoreT_ps = sem("scoreT_ps")
        scoreT_ready = sem("scoreT_ready")
        acc0_ps = sem("acc0_ps")
        acc_ready = sem("acc_ready")
        hmoe_ps = sem("hmoe_ps")
        hmoe_ready = sem("hmoe_ready")
        ymoe_ps = sem("ymoe_ps")
        ymoe_used = sem("ymoe_used")
        qkv_ps = sem("qkv_ps")
        split_ready = sem("split_ready")
        v_ready = sem("v_ready")
        vsrc_ready = sem("vsrc_ready")
        tqk_ps = sem("tqk_ps")
        kT_ready = sem("kT_ready")
        qT_ready = sem("qT_ready")
        diag_ready = sem("diag_ready")
        smax_ps = sem("smax_ps")
        smax_used = sem("smax_used")
        mneg_ready = sem("mneg_ready")
        mT_ps = sem("mT_ps")
        mT_ready = sem("mT_ready")
        shift_ready = sem("shift_ready")
        s_ps = sem("s_ps")
        probs_ready = sem("probs_ready")
        pv_done = sem("pv_done")
        oT_ready = sem("oT_ready")
        oN_ps = sem("oN_ps")
        yn_ready = sem("yn_ready")
        yT_ps = sem("yT_ps")
        yT_ready = sem("yT_ready")
        proj_ps = sem("proj_ps")
        proj_used = sem("proj_used")
        y_ready = sem("y_ready")
        dve_step = sem("dve_step")
        pool_step = sem("pool_step")
        of_a_batch = range(ssq_ready.num, pool_step.num + 1)

        loads = [
            (x_all[:], a["x"].rearrange("b (t p) d -> p (b t) d", p=P)),
            (wkvr[:], a["wkvr"].rearrange("c i o -> i c o")), (wo0[:], a["wo0"]), (wfc[:], a["wfc"]),
            (wmlp[:], a["wmlp"].rearrange("(c p) d -> p c d", p=P)), (wg[:], a["wg"]),
            (w1[:], a["w1"].rearrange("e i o -> i e o")), (b1[:], a["b1"].rearrange("e (c p) -> p e c", p=P)),
            (w2[:], a["w2"].rearrange("e (c p) d -> p e c d", p=P)), (b2[:], a["b2"]),
            (wqkv[:], a["wqkv"].rearrange("u i o -> i u o")), (bqkv[:], a["bqkv"].partition_broadcast(P)),
            (wproj[:], a["wproj"].rearrange("u i o -> i u o")), (bproj[:], a["bproj"].partition_broadcast(P)),
            (bo[:], a["bo"]), (qk_w[:], a["qk_w"].partition_broadcast(P)), (router_w[:], a["router_w"]),
            (router_b[:], a["router_b"].partition_broadcast(P)), (decay[:], a["decay"]),
            (mixer_scale[:], a["mixer_scale"].partition_broadcast(P)),
            (mlp_scale[:], a["mlp_scale"].partition_broadcast(P)),
        ]
        CONSTS = 11

        def end_batch(eng):
            eng.drain().then_inc(batch_done, 1)
            eng.wait_ge(cleared, 1)
            eng.sem_inc(passed, 1)

        block = ctx.enter_context(nc.Block())

        @block.sync
        def _(sp):
            for dst, src in loads:
                sp.dma_start(dst, src, allow_slow_non_contiguous=True).then_inc(loaded, 16)
            with sp.Fori(0, B) as b:
                for u in range(U):
                    sp.wait_ge(qT_ready, u + 1)
                    for j in range(J):
                        sp.dma_start(q_diag[SLOT * j:SLOT * (j + 1), j, :, :],
                                     qT[SLOT * j:SLOT * (j + 1), :, :]).then_inc(diag_ready, 16)
                    sp.wait_ge(mT_ready, u + 1)
                    for j in range(J):
                        row = SLOT * j + SHIFT_ROW
                        sp.dma_start(q_diag[row:row + 1, j, :, :], mT[j:H:J, :]).then_inc(shift_ready, 16)
                sp.wait_ge(y_ready, 1)
                sp.dma_start(out[bass.ds(b, 1), :, :].rearrange("b (t p) d -> p (b t) d", p=P),
                             y_all[:, bass.ds(b * T, T), :]).then_inc(stored, 16)
                end_batch(sp)
            sp.wait_ge(stored, 16 * B)

        @block.gpsimd
        def _(pool):
            pool.memset(ident[:], 0.0).then_inc(const_ready, 1)
            pool.memset(q_diag[:], 0.0).then_inc(const_ready, 1)
            pool.memset(q_split[:], 0.0).then_inc(const_ready, 1)
            pool.memset(k_split[:], 0.0).then_inc(const_ready, 1)
            pool.memset(v_ext[:], 0.0).then_inc(const_ready, 1)
            pool.memset(half[:], -0.5).then_inc(const_ready, 1)
            for e in range(E0):
                pool.memset(prio[:, e:e + 1], float(E0 - e))
            pool.memset(state[:, 0:1], 0.0).then_inc(const_ready, 1)
            pool.wait_ge(const_ready, 7)
            pool.affine_select(out=ident[:], in_=ident[:], compare_op=ALU.not_equal, fill=1.0, base=0,
                               pattern=[[-1, P]], channel_multiplier=1).then_inc(const_ready, 1)
            pool.memset(q_split[:, :, :, MASK_ROW:MASK_ROW + 1], 1.0).then_inc(const_ready, 1)
            pool.memset(k_split[:, :, :, SHIFT_ROW:SHIFT_ROW + 1], 1.0).then_inc(const_ready, 1)
            pool.memset(v_ext[:, :, :, HD:HD + 1], 1.0).then_inc(const_ready, 1)
            pool.wait_ge(const_ready, CONSTS)

            with pool.Fori(0, B) as b:
                steps = [0]

                def link(ins):
                    steps[0] += 1
                    ins.then_inc(pool_step, 1)
                    pool.wait_ge(pool_step, steps[0])

                def inverse_root(dst, work, src, scale, eps):
                    link(pool.tensor_scalar(work, src, scale, eps, ALU.mult, ALU.add))
                    pool.tensor_tensor(dst, work, half[:, 0:T], ALU.pow).then_inc(rstd_ready, 1)

                for i in range(2):
                    pool.wait_ge(ssq_ready, i + 1)
                    inverse_root(rstd[:, i, :], var[:, i, :], ssq[:, i, :], 1.0 / D, RMS_EPS)
                for i in range(2):
                    pool.wait_ge(lnvar_ready, i + 1)
                    inverse_root(rstd[:, 2 + i, :], var[:, 2 + i, :], mv[:, i, :, 1], 1.0, LN_EPS)
                for u in range(U):
                    if u == 0:
                        pool.wait_ge(qkms_ready, 1)
                        link(pool.tensor_scalar(ms[:], ms[:], 1.0 / HD, RMS_EPS, ALU.mult, ALU.add))
                        pool.tensor_tensor(rqk[:], ms[:], half[:, 0:2 * T * H], ALU.pow).then_inc(rstd_ready, 1)
                    pool.wait_ge(vsrc_ready, u + 1)
                    pool.tensor_copy(v_ext[:, :, :, 0:HD],
                                     qkv[:, 2, :, :].rearrange("p t (h d) -> p t h d", h=H)).then_inc(v_ready, 1)
                    if u == 0:
                        pool.wait_ge(lnvar_ready, 3)
                        inverse_root(rstd[:, 4, :], var[:, 4, :], mv[:, 2, :, 1], 1.0, LN_EPS)
                pool.wait_ge(lnvar_ready, 4)
                inverse_root(rstd[:, 5, :], var[:, 5, :], mv[:, 3, :, 1], 1.0, LN_EPS)
                pool.drain().then_inc(batch_done, 1)
                pool.wait_ge(batch_done, 5)
                pool.sem_clear(of_a_batch)
                pool.sem_clear(batch_done)
                pool.sem_inc(cleared, 1)
                pool.wait_ge(passed, 4)
                pool.sem_clear(passed)
                pool.sem_clear(cleared)

        @block.scalar
        def _(act):
            act.wait_ge(loaded, 16 * len(loads))
            act.activation(ew[:, 0:1], decay[:, 0:1], ACT.Exp).then_inc(exp_decay, 1)
            act.wait_ge(exp_decay, 1)
            act.activation(decay[:, 0:1], ew[:, 0:1], ACT.Exp, scale=-1.0).then_inc(exp_decay, 1)
            act.activation(ew[:, 1:2], decay[:, 1:2], ACT.Exp).then_inc(exp_decay, 1)

            with act.Fori(0, B) as b:
                for t in range(T):
                    last = act.activation(junk[:, 0, t, :], x_all[:, bass.ds(b * T + t, 1), :].rearrange("p a d -> p (a d)"),
                                          ACT.Square, accum_out=ssq[:, 0, t:t + 1])
                last.then_inc(ssq_ready, 1)
                act.wait_ge(xT_ps, 1)
                act.copy(xT[:], m0[:, 0:S]).then_inc(xT_ready, 1)
                act.wait_ge(kvr_ps, 1)
                act.copy(k_sb[:], ps[:, 0, 0:S]).then_inc(k_sb_ready, 1)
                act.wait_ge(kvr_ps, 3)
                act.activation(er[:], ps[:, 2, 0:S], ACT.Exp, scale=-1.0).then_inc(er_ready, 1)
                act.wait_ge(x1_ready, 1)
                for t in range(T):
                    last = act.activation(junk[:, 1, t, :], x1[:, t, :], ACT.Square, accum_out=ssq[:, 1, t:t + 1])
                last.then_inc(ssq_ready, 1)
                act.wait_ge(xT_ps, 2)
                act.copy(xT[:], m0[:, 0:S]).then_inc(xT_ready, 1)
                act.wait_ge(fc_ps, 1)
                act.activation(z_half[:].rearrange("p c s -> p (c s)"), s_buf[0].rearrange("p a b -> p (a b)"),
                               ACT.Copy, scale=0.5).then_inc(zhalf_ready, 1)

                def softmax_exp(i):
                    act.wait_ge(lg_ready, i + 1)
                    act.activation(pr[:, :, 0:(E0, E1)[i]], lg[:, :, 0:(E0, E1)[i]], ACT.Exp).then_inc(pexp_ready, 1)

                def score_rows(i, n_e):
                    act.wait_ge(scoreT_ps, i + 1)
                    act.copy(scoreT[0:n_e, :], m0[0:n_e, 0:S]).then_inc(scoreT_ready, 1)

                act.wait_ge(xT_ps, 3)
                act.copy(xT[:], m0[:, 0:S]).then_inc(xT_ready, 1)
                softmax_exp(0)
                score_rows(0, E0)
                for e in range(E0):
                    act.wait_ge(hmoe_ps, e + 1)
                    for c in range(HB):
                        last = act.activation(h_moe[:, e % 2, c, :], ps[:, e % 2, c * S:(c + 1) * S], ACT.Relu,
                                              bias=b1[:, e, c:c + 1])
                    last.then_inc(hmoe_ready, 1)
                act.wait_ge(xT_ps, 4)
                act.copy(xT[:], m0[:, 0:S]).then_inc(xT_ready, 1)
                for u in range(U):
                    if u == 1:
                        act.wait_ge(xT_ps, 5)
                        act.copy(xT[:], m0[:, 0:S]).then_inc(xT_ready, 1)
                        softmax_exp(1)
                        score_rows(1, E1)
                    act.wait_ge(tqk_ps, 2 * u + 2)
                    act.copy(qT[:].rearrange("p g s -> p (g s)"), m1.bitcast(F16)[:, 0:G * S]).then_inc(qT_ready, 1)
                    act.wait_ge(mT_ps, u + 1)
                    act.copy(mT[:], m0.bitcast(F16)[0:H, 0:S]).then_inc(mT_ready, 1)
                    for i in range(G * T):
                        act.wait_ge(s_ps, u * (G * T) + i + 1)
                        act.activation(probs[:, i % 2, :, :].rearrange("p j s -> p (j s)"),
                                       s_buf[i % 2].rearrange("p a b -> p (a b)"), ACT.Exp,
                                       scale=HD ** -0.5 if u == 0 else 0.5).then_inc(probs_ready, 1)
                    act.wait_ge(pv_done, u * (G * T) + G * T)
                    act.copy(oT[:].rearrange("p g s -> p (g s)"), o_ps.rearrange("p g s -> p (g s)")).then_inc(oT_ready, 1)
                    act.wait_ge(yT_ps, u + 1)
                    act.copy(yT[:], m0[:, 0:S]).then_inc(yT_ready, 1)
                end_batch(act)

        @block.vector
        def _(v):
            v.wait_ge(exp_decay, 3)
            v.wait_ge(const_ready, CONSTS)
            v.tensor_copy(ident16[:], ident[:]).then_inc(ew_ready, 1)
            v.tensor_scalar(ew_bc[:], decay[:, 0:1].broadcast_to([D, S]), 1.0, None, ALU.mult).then_inc(ew_ready, 1)
            v.wait_ge(ew_ready, 2)

            with v.Fori(0, B) as b:
                steps = [0]

                def link(ins):
                    steps[0] += 1
                    ins.then_inc(dve_step, 1)
                    v.wait_ge(dve_step, steps[0])

                xb = x_all[:, bass.ds(b * T, T), :]

                def layer_norm(i, src, dst, dst_sem):
                    for t in range(T):
                        link(v.bn_stats(bn6[:, t, :], src[:, t, :]))
                    v.bn_aggr(mv[:, i, 0, :], bn6[:, 0, :])
                    v.bn_aggr(mv[:, i, 1, :], bn6[:, 1, :]).then_inc(lnvar_ready, 1)
                    v.wait_ge(rstd_ready, (3, 4, 6, 7)[i])
                    for t in range(T):
                        last = v.tensor_scalar(dst[:, t, :], src[:, t, :], mv[:, i, t, 0:1], rstd[:, 2 + i, t:t + 1],
                                               ALU.subtract, ALU.mult)
                    last.then_inc(dst_sem, 1)

                def bc(x, n):
                    return x.unsqueeze(2).broadcast_to([P, T, n])

                def top2(i, n_e, bias):
                    e_ = slice(0, n_e)
                    v.wait_ge(logit_ps, i + 1)
                    src = m0.rearrange("p (t x) -> p t x", t=T)[:, :, e_]
                    if bias is not None:
                        link(v.tensor_tensor(lg[:, :, e_], src, bias[:].unsqueeze(1).broadcast_to([P, T, n_e]), ALU.add))
                    else:
                        link(v.tensor_copy(lg[:, :, e_], src))
                    link(v.reduce_max(st1[:, 0, :], lg[:, :, e_], AX))
                    v.tensor_tensor(lg[:, :, e_], lg[:, :, e_], bc(st1[:, 0, :], n_e), ALU.subtract).then_inc(lg_ready, 1)
                    v.wait_ge(pexp_ready, i + 1)
                    link(v.reduce_sum(st1[:, 1, :], pr[:, :, e_], AX))
                    link(v.reciprocal(st1[:, 2, :], st1[:, 1, :]))
                    link(v.tensor_tensor(pr[:, :, e_], pr[:, :, e_], bc(st1[:, 2, :], n_e), ALU.mult))
                    pb = prio[:, e_].unsqueeze(1).broadcast_to([P, T, n_e])

                    def first_largest(src, top, one_hot):
                        link(v.reduce_max(top, src[:, :, e_], AX))
                        link(v.tensor_tensor(tk[:, :, e_], src[:, :, e_], bc(top, n_e), ALU.is_equal))
                        link(v.tensor_tensor(tk[:, :, e_], tk[:, :, e_], pb, ALU.mult))
                        link(v.reduce_max(st1[:, 5, :], tk[:, :, e_], AX))
                        link(v.tensor_tensor(one_hot[:, :, e_], bc(st1[:, 5, :], n_e), pb, ALU.is_equal))

                    first_largest(pr, st1[:, 3, :], oh1)
                    link(v.scalar_tensor_tensor(lg[:, :, e_], oh1[:, :, e_], -2.0, pr[:, :, e_], ALU.mult, ALU.add))
                    first_largest(lg, st1[:, 4, :], oh2)
                    link(v.tensor_tensor(oh1[:, :, e_], oh1[:, :, e_], oh2[:, :, e_], ALU.add))

                v.wait_ge(rstd_ready, 1)
                for t in range(T):
                    last = v.tensor_scalar(xn[:, t, :], x_all[:, bass.ds(b * T + t, 1), :].rearrange("p a d -> p (a d)"),
                                           rstd[:, 0, t:t + 1], None, ALU.mult)
                last.then_inc(xn_ready, 1)
                v.wait_ge(k_sb_ready, 1)
                v.wait_ge(kvr_ps, 2)
                link(v.tensor_tensor(kv[:], k_sb[:], ps[:, 1, 0:S], ALU.mult))
                link(v.tensor_tensor_scan(state[:, 1:S + 1], ew_bc[:], kv[:], 0.0, ALU.mult, ALU.add))
                link(v.scalar_tensor_tensor(kv[:], kv[:], ew[:, 1:2], state[:, 0:S], ALU.mult, ALU.add))
                v.wait_ge(er_ready, 1)
                link(v.tensor_scalar(gate[:], er[:], 1.0, None, ALU.add))
                link(v.reciprocal(gate[:], gate[:]))
                v.tensor_tensor(mixT[:], kv[:], gate[:], ALU.mult).then_inc(mixT_ready, 1)
                v.wait_ge(mix_ps, 1)
                msc = mixer_scale[:].unsqueeze(1).broadcast_to([P, T, D])
                link(v.tensor_tensor(tmp[:], m1[:, 0:T * D].rearrange("p (t d) -> p t d", t=T), msc, ALU.mult))
                v.tensor_tensor(x1[:], tmp[:], xb, ALU.add).then_inc(x1_ready, 1)
                v.wait_ge(rstd_ready, 2)
                for t in range(T):
                    last = v.tensor_scalar(xn[:, t, :], x1[:, t, :], rstd[:, 1, t:t + 1], None, ALU.mult)
                last.then_inc(xn_ready, 1)
                v.wait_ge(zhalf_ready, 1)
                hf, zf = h_fc[:].rearrange("p c s -> p (c s)"), z_half[:].rearrange("p c s -> p (c s)")
                link(v.tensor_tensor(hf, zf, s_buf[0].rearrange("p a b -> p (a b)"), ALU.max))
                v.tensor_tensor(hf, hf, hf, ALU.mult).then_inc(hfc_ready, 1)
                v.wait_ge(mlp_ps, 1)
                lsc = mlp_scale[:].unsqueeze(1).broadcast_to([P, T, D])
                link(v.tensor_tensor(tmp[:], m1[:, 0:T * D].rearrange("p (t d) -> p t d", t=T), lsc, ALU.mult))
                link(v.tensor_tensor(tmp[:], tmp[:], x1[:], ALU.add))
                link(v.tensor_tensor(tmp[:], tmp[:], xb, ALU.add))
                layer_norm(0, tmp, x3, xn_ready)
                v.wait_ge(xn_ready, 3)

                top2(0, E0, None)
                link(v.tensor_tensor(score[:], oh1[:], pr[:], ALU.mult))
                link(v.reduce_sum(st1[:, 6, :], score[:], AX))
                link(v.reciprocal(st1[:, 7, :], st1[:, 6, :]))
                v.tensor_tensor(score[:], score[:], bc(st1[:, 7, :], E0), ALU.mult).then_inc(score_ready, 1)
                v.wait_ge(score_ready, 1)
                v.wait_ge(acc0_ps, 1)
                link(v.tensor_tensor(acc[:], m1[:, 0:T * D].rearrange("p (t d) -> p t d", t=T), x3[:], ALU.add))
                for e in range(E0):
                    v.wait_ge(ymoe_ps, e + 1)
                    for t in range(T):
                        last = v.scalar_tensor_tensor(acc[:, t, :], ps[:, 2 + e % 2, t * D:(t + 1) * D],
                                                      score[:, t, e:e + 1], acc[:, t, :], ALU.mult, ALU.add)
                    last.then_inc(ymoe_used, 1)
                    v.wait_ge(ymoe_used, e + 1)
                layer_norm(1, acc, x4, xn_ready)

                for u in range(U):
                    if u == 1:
                        v.wait_ge(xn_ready, 5)
                        top2(1, E1, router_b)
                        link(v.tensor_copy(member[:], oh1[:, :, 0:E1]))
                        link(v.tensor_scalar(key_mask[:], member[:], -MASKED, MASKED, ALU.mult, ALU.add))
                        v.tensor_tensor(w_tok[:], member[:], pr[:, :, 0:E1], ALU.mult).then_inc(score_ready, 1)
                        v.wait_ge(score_ready, 2)
                        v.wait_ge(acc0_ps, 2)
                        v.tensor_tensor(acc[:], m1[:, 0:T * D].rearrange("p (t d) -> p t d", t=T), x3[:],
                                        ALU.add).then_inc(acc_ready, 1)
                        v.wait_ge(acc_ready, 1)
                    v.wait_ge(qkv_ps, u + 1)
                    bias = bqkv[:, u, :].rearrange("p (c d) -> p c d", c=3)
                    for t in range(T):
                        last = v.tensor_tensor(qkv[:, :, t, :], both[:, t, 0:3 * D].rearrange("p (c d) -> p c d", c=3),
                                               bias, ALU.add)
                    last.then_inc(vsrc_ready, 1)
                    v.wait_ge(vsrc_ready, u + 1)
                    if u == 0:
                        link(v.tensor_tensor(sq[:], qkv[:, 0:2], qkv[:, 0:2], ALU.mult))
                        v.reduce_sum(ms[:], sq[:].rearrange("p c t (h d) -> p (c t h) d", h=H), AX).then_inc(qkms_ready, 1)
                        v.wait_ge(rstd_ready, 5)
                        qk = qkv[:, 0:2].rearrange("p c t (h d) -> p (c t h) d", h=H)
                        link(v.tensor_tensor(qk, qk, rqk[:].unsqueeze(2).broadcast_to([P, 2 * T * H, HD]), ALU.mult))
                        for c in range(2):
                            qc = qkv[:, c].rearrange("p t (h d) -> p (t h) d", h=H)
                            link(v.tensor_tensor(qc, qc, qk_w[:, c, :].unsqueeze(1).broadcast_to([P, T * H, HD]), ALU.mult))
                    qf = qkv[:, 0].rearrange("p t (h d) -> p (t h) d", h=H)
                    kf = qkv[:, 1].rearrange("p t (h d) -> p (t h) d", h=H)
                    qs = q_split[:].rearrange("p t h s -> p (t h) s")
                    ks = k_split[:].rearrange("p t h s -> p (t h) s")

                    def part(x, c):
                        return x[:, :, c * HD:(c + 1) * HD]
                    link(v.tensor_copy(part(qs, 0), qf))
                    link(v.tensor_copy(part(qs, 1), qf))
                    link(v.tensor_tensor(part(qs, 2), qf, part(qs, 0), ALU.subtract))
                    link(v.tensor_copy(part(ks, 0), kf))
                    link(v.tensor_copy(part(ks, 2), kf))
                    if u > 0:
                        link(v.tensor_copy(k_split[:, :, :, MASK_ROW], bc(key_mask[:, :, u - 1], H)))
                    else:
                        link(v.memset(k_split[:, :, :, MASK_ROW:MASK_ROW + 1], 0.0))
                    v.tensor_tensor(part(ks, 1), kf, part(ks, 0), ALU.subtract).then_inc(split_ready, 1)
                    v.wait_ge(tqk_ps, 2 * u + 1)
                    v.tensor_copy(kT[:].rearrange("p g s -> p (g s)"), m0.bitcast(F16)[:, 0:G * S]).then_inc(kT_ready, 1)
                    for i in range(G * T):
                        t, g = i // G, i % G
                        v.wait_ge(smax_ps, u * (G * T) + i + 1)
                        v.reduce_max(mx[:, t, J * g:J * (g + 1)],
                                     s_buf[i % 2].rearrange("p a (c k) -> p (a c) k", c=2), AX).then_inc(smax_used, 1)
                    v.wait_ge(smax_used, (u + 1) * (G * T))
                    v.tensor_scalar(mneg[:], mx[:], -1.0, None, ALU.mult).then_inc(mneg_ready, 1)
                    v.wait_ge(oN_ps, u + 1)
                    oN = both.rearrange("p t (h s) -> p t h s", h=H)
                    link(v.reciprocal(rden[:], oN[:, :, :, HD]))
                    if u > 0:
                        link(v.tensor_tensor(rden[:], rden[:], bc(w_tok[:, :, u - 1], H), ALU.mult))
                    v.tensor_tensor(y_n[:].rearrange("p t (h d) -> p (t h) d", h=H),
                                    both.rearrange("p t (h s) -> p (t h) s", h=H)[:, :, 0:HD],
                                    rden[:].rearrange("p t h -> p (t h)").unsqueeze(2).broadcast_to([P, T * H, HD]),
                                    ALU.mult).then_inc(yn_ready, 1)
                    v.wait_ge(proj_ps, u + 1)
                    pj = m1[:, 0:T * D].rearrange("p (t d) -> p t d", t=T)
                    if u == 0:
                        v.tensor_tensor(tmp[:], pj, bproj[:].unsqueeze(1).broadcast_to([P, T, D]),
                                        ALU.add).then_inc(proj_used, 1)
                        v.wait_ge(proj_used, u + 1)
                        link(v.tensor_tensor(tmp[:], tmp[:], x4[:], ALU.add))
                        layer_norm(2, tmp, x3, xn_ready)
                    else:
                        v.tensor_tensor(acc[:], acc[:], pj, ALU.add).then_inc(proj_used, 1)
                        v.wait_ge(proj_used, u + 1)
                layer_norm(3, acc, y_all[:, bass.ds(b * T, T), :], y_ready)
                end_batch(v)

        @block.tensor
        def _(pe):
            pe.wait_ge(loaded, 16 * len(loads))
            pe.wait_ge(ew_ready, 2)

            with pe.Fori(0, B) as b:
                def transpose_tiles(dst, src, k, done_sem):
                    for t in range(T):
                        last = pe.transpose(dst[:, t * P:(t + 1) * P], src[:, t, :], ident[:])
                    last.then_inc(done_sem, 1)

                def to_rows(i):
                    pe.wait_ge(xn_ready, i)
                    transpose_tiles(m0, (xn, xn, x3, x4, x3)[i - 1], i, xT_ps)
                    pe.wait_ge(xT_ready, i)

                def mm(o, l, r, start=True, stop=True):
                    return pe.matmul(o, l, r, start=start, stop=stop)

                to_rows(1)
                for c in range(3):
                    mm(ps[:, c, 0:S], wkvr[:, c, :], xT[:]).then_inc(kvr_ps, 1)
                pe.wait_ge(mixT_ready, 1)
                for t in range(T):
                    last = mm(m1[:, t * D:(t + 1) * D], mixT[:, t * P:(t + 1) * P], wo0[:])
                last.then_inc(mix_ps, 1)
                to_rows(2)
                for c in range(FC):
                    last = mm(ps[:, c // 2, (c % 2) * S:(c % 2 + 1) * S], wfc[:, c * P:(c + 1) * P], xT[:])
                last.then_inc(fc_ps, 1)
                pe.wait_ge(hfc_ready, 1)
                for t in range(T):
                    for c in range(FC):
                        last = mm(m1[:, t * D:(t + 1) * D], h_fc[:, c, t * P:(t + 1) * P], wmlp[:, c, :],
                                  start=c == 0, stop=c == FC - 1)
                last.then_inc(mlp_ps, 1)

                def route(i, n_e, w, s_tile, w_bias):
                    for t in range(T):
                        last = mm(m0[:, t * S:t * S + n_e], xT[:, t * P:(t + 1) * P], w[:])
                    last.then_inc(logit_ps, 1)
                    pe.wait_ge(score_ready, i + 1)
                    for t in range(T):
                        last = pe.transpose(m0[0:n_e, t * P:(t + 1) * P], s_tile[:, t, 0:n_e], ident[:])
                    last.then_inc(scoreT_ps, 1)
                    pe.wait_ge(scoreT_ready, i + 1)
                    for t in range(T):
                        last = mm(m1[:, t * D:(t + 1) * D], scoreT[0:n_e, t * P:(t + 1) * P], w_bias[:])
                    last.then_inc(acc0_ps, 1)

                to_rows(3)
                route(0, E0, wg, score, b2)
                for e in range(E0 + 1):
                    if e < E0:
                        if e >= 2:
                            pe.wait_ge(hmoe_ready, e - 1)
                        for c in range(HB):
                            last = mm(ps[:, e % 2, c * S:(c + 1) * S], w1[:, e, c * P:(c + 1) * P], xT[:])
                        last.then_inc(hmoe_ps, 1)
                    if e >= 1:
                        f = e - 1
                        pe.wait_ge(hmoe_ready, f + 1)
                        if f >= 2:
                            pe.wait_ge(ymoe_used, f - 1)
                        for t in range(T):
                            for c in range(HB):
                                last = mm(ps[:, 2 + f % 2, t * D:(t + 1) * D], h_moe[:, f % 2, c, t * P:(t + 1) * P],
                                          w2[:, f, c, :], start=c == 0, stop=c == HB - 1)
                        last.then_inc(ymoe_ps, 1)
                to_rows(4)
                for u in range(U):
                    if u == 1:
                        to_rows(5)
                        route(1, E1, router_w, w_tok, bo)
                    if u == 1:
                        pe.wait_ge(acc_ready, 1)
                    elif u >= 2:
                        pe.wait_ge(proj_used, u)
                    for t in range(T):
                        last = mm(both[:, t, 0:3 * D], xT[:, t * P:(t + 1) * P], wqkv[:, u, :])
                    last.then_inc(qkv_ps, 1)
                    pe.wait_ge(split_ready, u + 1)
                    for dst, src in ((m0, k_split), (m1, q_split)):
                        for g in range(G):
                            for t in range(T):
                                last = pe.transpose(dst.bitcast(F16)[:, g * S + t * P:g * S + (t + 1) * P],
                                                    src[:, t, J * g:J * (g + 1), :].rearrange("p h s -> p (h s)"),
                                                    ident16[:])
                        last.then_inc(tqk_ps, 1)
                    pe.wait_ge(kT_ready, u + 1)
                    pe.wait_ge(diag_ready, (u + 1) * (16 * J))
                    for i in range(G * T):
                        t, g = i // G, i % G
                        if i >= 2:
                            pe.wait_ge(smax_used, u * (G * T) + i - 1)
                        for j in range(J):
                            last = mm(s_buf[i % 2][:, j // 2, (j % 2) * S:(j % 2 + 1) * S],
                                      q_diag[:, j, g, t * P:(t + 1) * P], kT[:, g, :])
                        last.then_inc(smax_ps, 1)
                    pe.wait_ge(mneg_ready, u + 1)
                    for t in range(T):
                        last = pe.transpose(m0.bitcast(F16)[0:H, t * P:(t + 1) * P], mneg[:, t, :], ident16[:])
                    last.then_inc(mT_ps, 1)
                    pe.wait_ge(shift_ready, (u + 1) * (16 * J))
                    pe.wait_ge(v_ready, u + 1)

                    def scores(i):
                        g, t = i // T, i % T
                        if i >= 2:
                            pe.wait_ge(probs_ready, u * (G * T) + i - 1)
                        for c in range(2):
                            last = mm(s_buf[i % 2][:, c, :], kT[:, g, t * P:(t + 1) * P], q_diag[:, 2 * c:2 * c + 2, g, :])
                        last.then_inc(s_ps, 1)

                    def weigh(i):
                        g, t = i // T, i % T
                        pe.wait_ge(probs_ready, u * (G * T) + i + 1)
                        for j in range(J):
                            last = mm(o_ps[SLOT * j:SLOT * (j + 1), g, :], v_ext[:, t, J * g + j, :], probs[:, i % 2, j, :],
                                      start=t == 0, stop=t == T - 1)
                        last.then_inc(pv_done, 1)

                    scores(0)
                    for i in range(G * T):
                        if i + 1 < G * T:
                            scores(i + 1)
                        weigh(i)
                    pe.wait_ge(oT_ready, u + 1)
                    for t in range(T):
                        for g in range(G):
                            last = pe.transpose(both[:, t, g * P:(g + 1) * P], oT[:, g, t * P:(t + 1) * P], ident[:])
                    last.then_inc(oN_ps, 1)
                    pe.wait_ge(yn_ready, u + 1)
                    transpose_tiles(m0, y_n, u, yT_ps)
                    pe.wait_ge(yT_ready, u + 1)
                    for t in range(T):
                        last = mm(m1[:, t * D:(t + 1) * D], yT[:, t * P:(t + 1) * P], wproj[:, u, :])
                    last.then_inc(proj_ps, 1)
                end_batch(pe)


def kernel(**inputs):
    import concourse.bacc as bacc
    from concourse.bass_utils import run_bass_kernel_spmd

    f = {k: np.ascontiguousarray(v) for k, v in inputs.items()}
    c = np.ascontiguousarray
    a = {
        "x": f["L0_attn_x"],
        "wkvr": c(np.stack([f["L0_attn_Wk"].T, f["L0_attn_Wv"].T, f["L0_attn_Wr"].T])),
        "wo0": c(f["L0_attn_Wo"].T),
        "decay": c(np.stack([f["L0_attn_time_decay"], f["L0_attn_time_first"]], axis=1)),
        "mixer_scale": f["L0_attn_mixer_scale"],
        "wfc": c(f["L0_attn_Wfc"].T),
        "wmlp": c(f["L0_attn_Wmlp"].T),
        "mlp_scale": f["L0_attn_mlp_scale"],
        "wg": f["L0_ffn_Wg"], "w1": f["L0_ffn_W1"], "b1": f["L0_ffn_b1"], "w2": f["L0_ffn_W2"], "b2": f["L0_ffn_b2"],
        "wqkv": c(np.concatenate([f["L1_attn_W_qkv"][None],
                                  np.concatenate([f["L1_ffn_wq"], f["L1_ffn_wk"], f["L1_ffn_wv"]], axis=2)])),
        "bqkv": c(np.concatenate([f["L1_attn_b_qkv"][None],
                                  np.concatenate([f["L1_ffn_bq"], f["L1_ffn_bk"], f["L1_ffn_bv"]], axis=1)])),
        "wproj": c(np.concatenate([f["L1_attn_W_proj"][None], f["L1_ffn_wo"]])),
        "bproj": f["L1_attn_b_proj"],
        "bo": f["L1_ffn_bo"],
        "qk_w": c(np.stack([f["L1_attn_qn_w"], f["L1_attn_kn_w"]])),
        "router_w": f["L1_ffn_router_w"], "router_b": f["L1_ffn_router_b"],
    }
    nc = bacc.Bacc("TRN2", target_bir_lowering=False, num_devices=1)
    aps = {k: nc.dram_tensor("in_" + k, v.shape, F32, kind="ExternalInput").ap() for k, v in a.items()}
    out = nc.dram_tensor("out_0", (B, S, D), F32, kind="ExternalOutput").ap()
    program(nc, aps, out)
    r = run_bass_kernel_spmd(nc, [{"in_" + k: v for k, v in a.items()}], core_ids=[0])
    return r.results[0]["out_0"]
```

```python
import numpy as np
import concourse.bass as bass
from concourse import mybir
from contextlib import ExitStack

F32 = mybir.dt.float32
F16 = mybir.dt.float16
ALU = mybir.AluOpType
ACT = mybir.ActivationFunctionType
AX = mybir.AxisListType.X

B, S, D = 16, 256, 128
P = 128
T = S // P
CB = 2
CT, CS = CB * T, CB * S
CHUNKS = B // CB
FC = 4 * D // P
E0, HB = 8, 2
E1 = 4
H, HD = 16, 8
G, J = 4, 4
SLOT = P // J
U = 1 + E1
HALVES = G * T * 2
LEAD = 5
RMS_EPS, LN_EPS = 1e-6, 1e-5
MASKED = -60000.0
DMA = 16

SHIFT_ROW, MASK_ROW = 3 * HD, 3 * HD + 1


class Unit:

    def __init__(self, sig, u, n, parity):
        self.s, self.u, self.n, self.parity = sig, u, n, parity


class LayerZeroSignals:

    def __init__(self, sem):
        self.ssq_ready = sem("ssq_ready")
        self.rstd_ready = sem("rstd_ready")
        self.xn_ready = sem("xn_ready")
        self.xT_ps = sem("xT_ps")
        self.xT_ready = sem("xT_ready")
        self.k_ps = sem("k_ps")
        self.k_sb_ready = sem("k_sb_ready")
        self.v_ps = sem("v_ps")
        self.r_ps = sem("r_ps")
        self.er_ready = sem("er_ready")
        self.kv_ready = sem("kv_ready")
        self.mixT_ready = sem("mixT_ready")
        self.mix_ps = sem("mix_ps")
        self.x1_ready = sem("x1_ready")
        self.fc_ps = sem("fc_ps")
        self.zhalf_ready = sem("zhalf_ready")
        self.h_ready = sem("h_ready")
        self.hfc_ready = sem("hfc_ready")
        self.mlp_ps = sem("mlp_ps")
        self.lnvar_ready = sem("lnvar_ready")
        self.logit_ps = sem("logit_ps")
        self.lg_ready = sem("lg_ready")
        self.pexp_ready = sem("pexp_ready")
        self.score_ready = sem("score_ready")
        self.scoreT_ps = sem("scoreT_ps")
        self.scoreT_ready = sem("scoreT_ready")
        self.acc0_ps = sem("acc0_ps")
        self.acc0_used = sem("acc0_used")
        self.acc_ready = sem("acc_ready")
        self.hmoe_ps = sem("hmoe_ps")
        self.hmoe_ready = sem("hmoe_ready")
        self.ymoe_ps = sem("ymoe_ps")
        self.ymoe_used = sem("ymoe_used")
        self.dve_step = sem("dve_step")
        self.pool_step = sem("pool_step")
        self.act_step = sem("act_step")
        self.numbers = range(self.ssq_ready.num, self.act_step.num + 1)


class GroupSignals:

    def __init__(self, sem):
        self.qkv_ps = sem("qkv_ps")
        self.qkv_ready = sem("qkv_ready")
        self.qkms_ready = sem("qkms_ready")
        self.rqk_ready = sem("rqk_ready")
        self.qn_ready = sem("qn_ready")
        self.v_ready = sem("v_ready")
        self.split_ready = sem("split_ready")
        self.tk_ps = sem("tk_ps")
        self.tq_ps = sem("tq_ps")
        self.kT_ready = sem("kT_ready")
        self.qT_ready = sem("qT_ready")
        self.diag_ready = sem("diag_ready")
        self.smax_ps = sem("smax_ps")
        self.smax_used = sem("smax_used")
        self.mneg_ready = sem("mneg_ready")
        self.mT_ps = sem("mT_ps")
        self.mT_ready = sem("mT_ready")
        self.shift_ready = sem("shift_ready")
        self.s_ps = sem("s_ps")
        self.probs_ready = sem("probs_ready")
        self.pv_done = sem("pv_done")
        self.oT_ready = sem("oT_ready")
        self.oN_ps = sem("oN_ps")
        self.yn_ready = sem("yn_ready")
        self.yT_ps = sem("yT_ps")
        self.yT_ready = sem("yT_ready")
        self.proj_ps = sem("proj_ps")
        self.proj_used = sem("proj_used")
        self.lnvar_ready = sem("lnvar_ready")
        self.rstd_ready = sem("rstd_ready")
        self.x5_ready = sem("x5_ready")
        self.x5T_ps = sem("x5T_ps")
        self.x5T_ready = sem("x5T_ready")
        self.logit_ps = sem("logit_ps")
        self.lg_ready = sem("lg_ready")
        self.pexp_ready = sem("pexp_ready")
        self.route_ready = sem("route_ready")
        self.scoreT_ps = sem("scoreT_ps")
        self.scoreT_ready = sem("scoreT_ready")
        self.acc0_ps = sem("acc0_ps")
        self.acc0_used = sem("acc0_used")
        self.x4_ready = sem("x4_ready")
        self.x4T_ps = sem("x4T_ps")
        self.x4T_ready = sem("x4T_ready")
        self.x4_used = sem("x4_used")
        self.y_ready = sem("y_ready")
        self.dve_step = sem("dve_step")
        self.pool_step = sem("pool_step")
        self.numbers = range(self.qkv_ps.num, self.pool_step.num + 1)


def program(nc, a, out):
    with ExitStack() as ctx:
        def sb(name, shape, dt=F32):
            return ctx.enter_context(nc.sbuf_tensor(name, shape, dt))

        def sem(name):
            return ctx.enter_context(nc.semaphore(name))

        wkvr = sb("wkvr", [D, 3, D])
        wo0 = sb("wo0", [D, D])
        wfc = sb("wfc", [D, FC * P])
        wmlp = sb("wmlp", [P, FC, D])
        wg = sb("wg", [D, E0])
        w1 = sb("w1", [D, E0, HB * P])
        b1 = sb("b1", [P, E0, HB])
        w2 = sb("w2", [P, E0, HB, D])
        b2 = sb("b2", [E0, D])
        wqkv = sb("wqkv", [D, U, 3 * D])
        bqkv = sb("bqkv", [P, U, 3 * D])
        wproj = sb("wproj", [D, U, D])
        bproj = sb("bproj", [P, D])
        bo = sb("bo", [E1, D])
        qk_w = sb("qk_w", [P, 2, HD])
        router_w = sb("router_w", [D, E1])
        router_b = sb("router_b", [P, E1])
        decay = sb("decay", [D, 2])
        mixer_scale = sb("mixer_scale", [P, D])
        mlp_scale = sb("mlp_scale", [P, D])
        ident = sb("ident", [P, P])
        ident16 = sb("ident16", [P, P], F16)
        half = sb("half", [P, 2 * T * H])
        prio = sb("prio", [P, E0])
        ew = sb("ew", [D, 2])
        ew_bc = sb("ew_bc", [D, S])

        x4_all = sb("x4_all", [P, B * T, D])

        ps = ctx.enter_context(nc.psum_tensor("ps", [P, 8, 512], F32))

        loaded = sem("loaded")
        const_ready = sem("const_ready")
        ew_ready = sem("ew_ready")
        exp_decay = sem("exp_decay")
        x_loaded = sem("x_loaded")
        stored = sem("stored")
        batch_done = sem("batch_done")
        cleared = sem("cleared")
        passed = sem("passed")
        done = [sem(f"done{p}") for p in range(2)]
        clean = [sem(f"clean{p}") for p in range(2)]
        l0 = LayerZeroSignals(lambda name: sem(f"{name}_l0"))
        sets = [GroupSignals(lambda name, p=p: sem(f"{name}_g{p}")) for p in range(2)]

        loads = [
            (wkvr[:], a["wkvr"].rearrange("c i o -> i c o")), (wo0[:], a["wo0"]), (decay[:], a["decay"]),
            (mixer_scale[:], a["mixer_scale"].partition_broadcast(P)), (wfc[:], a["wfc"]),
            (wmlp[:], a["wmlp"].rearrange("(c p) d -> p c d", p=P)), (wg[:], a["wg"]),
            (mlp_scale[:], a["mlp_scale"].partition_broadcast(P)),
            (w1[:], a["w1"].rearrange("e i o -> i e o")), (b1[:], a["b1"].rearrange("e (c p) -> p e c", p=P)),
            (w2[:], a["w2"].rearrange("e (c p) d -> p e c d", p=P)), (b2[:], a["b2"]),
            (wqkv[:], a["wqkv"].rearrange("u i o -> i u o")), (bqkv[:], a["bqkv"].partition_broadcast(P)),
            (wproj[:], a["wproj"].rearrange("u i o -> i u o")), (bproj[:], a["bproj"].partition_broadcast(P)),
            (bo[:], a["bo"]), (qk_w[:], a["qk_w"].partition_broadcast(P)), (router_w[:], a["router_w"]),
            (router_b[:], a["router_b"].partition_broadcast(P)),
        ]
        CONSTS = 3

        def meet(eng):
            eng.drain().then_inc(batch_done, 1)
            eng.wait_ge(cleared, 1)
            eng.sem_inc(passed, 1)

        def meet_and_clear(pool):
            pool.drain().then_inc(batch_done, 1)
            pool.wait_ge(batch_done, 4)
            pool.sem_clear(l0.numbers)
            pool.sem_clear(batch_done)
            pool.sem_inc(cleared, 1)
            pool.wait_ge(passed, 3)
            pool.sem_clear(passed)
            pool.sem_clear(cleared)

        def tiles(x, t=T):
            return x.rearrange("p (t d) -> p t d", t=t)

        def softmax_top2(v, link, sig, src, n_e, n_t, bias, lg, pr, tk, oh1, oh2, st, exp_count):
            def bc(x):
                return x.unsqueeze(2).broadcast_to([P, n_t, n_e])

            pb = prio[:, 0:n_e].unsqueeze(1).broadcast_to([P, n_t, n_e])

            def before_exp():
                if bias is not None:
                    link(v.tensor_tensor(lg, src, bias[:].unsqueeze(1).broadcast_to([P, n_t, n_e]), ALU.add))
                else:
                    link(v.tensor_copy(lg, src))
                link(v.reduce_max(st[:, 0, :], lg, AX))
                v.tensor_tensor(lg, lg, bc(st[:, 0, :]), ALU.subtract).then_inc(sig.lg_ready, 1)

            def first_largest(src, top, one_hot):
                link(v.reduce_max(top, src, AX))
                link(v.tensor_tensor(tk, src, bc(top), ALU.is_equal))
                link(v.tensor_tensor(tk, tk, pb, ALU.mult))
                link(v.reduce_max(st[:, 5, :], tk, AX))
                link(v.tensor_tensor(one_hot, bc(st[:, 5, :]), pb, ALU.is_equal))

            def after_exp():
                v.wait_ge(sig.pexp_ready, exp_count)
                link(v.reduce_sum(st[:, 1, :], pr, AX))
                link(v.reciprocal(st[:, 2, :], st[:, 1, :]))
                link(v.tensor_tensor(pr, pr, bc(st[:, 2, :]), ALU.mult))
                first_largest(pr, st[:, 3, :], oh1)
                link(v.scalar_tensor_tensor(lg, oh1, -2.0, pr, ALU.mult, ALU.add))

            def second():
                first_largest(lg, st[:, 4, :], oh2)
                link(v.tensor_tensor(oh1, oh1, oh2, ALU.add))

            return before_exp, after_exp, second

        with nc.Block() as block:
            @block.sync
            def _(sp):
                for dst, src in loads:
                    sp.dma_start(dst, src, allow_slow_non_contiguous=True).then_inc(loaded, DMA)

            @block.gpsimd
            def _(pool):
                pool.memset(ident[:], 0.0).then_inc(const_ready, 1)
                pool.memset(half[:], -0.5)
                for e in range(E0):
                    last = pool.memset(prio[:, e:e + 1], float(E0 - e))
                last.then_inc(const_ready, 1)
                pool.wait_ge(const_ready, 1)
                pool.affine_select(out=ident[:], in_=ident[:], compare_op=ALU.not_equal, fill=1.0, base=0,
                                   pattern=[[-1, P]], channel_multiplier=1).then_inc(const_ready, 1)
                pool.wait_ge(const_ready, CONSTS)

            @block.scalar
            def _(act):
                act.wait_ge(loaded, DMA * len(loads))
                act.activation(ew[:, 0:1], decay[:, 0:1], ACT.Exp).then_inc(exp_decay, 1)
                act.wait_ge(exp_decay, 1)
                act.activation(decay[:, 0:1], ew[:, 0:1], ACT.Exp, scale=-1.0).then_inc(exp_decay, 1)
                act.activation(ew[:, 1:2], decay[:, 1:2], ACT.Exp).then_inc(exp_decay, 1)

            @block.vector
            def _(v):
                v.wait_ge(const_ready, CONSTS)
                v.tensor_copy(ident16[:], ident[:]).then_inc(ew_ready, 1)
                v.wait_ge(exp_decay, 3)
                v.tensor_scalar(ew_bc[:], decay[:, 0:1].broadcast_to([D, S]), 1.0, None,
                                ALU.mult).then_inc(ew_ready, 1)

            @block.tensor
            def _(pe):
                pe.wait_ge(loaded, DMA * len(loads))
                pe.wait_ge(ew_ready, 2)

        with ExitStack() as ph:
            def sb1(name, shape, dt=F32):
                return ph.enter_context(nc.sbuf_tensor(name, shape, dt))

            x_all = sb1("x_all", [P, B * T, D])
            junk = sb1("junk", [P, 2, CT, D])
            ssq = sb1("ssq", [P, 2, CT])
            var = sb1("var", [P, 4, CT])
            rstd = sb1("rstd", [P, 4, CT])
            bn6 = sb1("bn6", [P, 2, CT, 6])
            mv = sb1("mv", [P, 2, CT, 2])
            xn = sb1("xn", [P, CT, D])
            xT = sb1("xT", [D, CS])
            x3T = sb1("x3T", [D, CS])
            k_sb = sb1("k_sb", [D, CS])
            er = sb1("er", [D, CS])
            gate = sb1("gate", [D, CS])
            kv = sb1("kv", [D, CS])
            wkv = sb1("wkv", [D, CS])
            state = sb1("state", [D, CB, S + 1])
            mixT = sb1("mixT", [D, CS])
            tmp = sb1("tmp", [P, CT, D])
            x1 = sb1("x1", [P, CT, D])
            z_half = sb1("z_half", [P, FC, CS])
            h_fc = sb1("h_fc", [P, FC, CS])
            x3 = sb1("x3", [P, 2, CT, D])
            acc = sb1("acc", [P, CT, D])
            h_moe = sb1("h_moe", [P, 2, HB, CS])
            lg = sb1("lg", [P, CT, E0])
            pr = sb1("pr", [P, CT, E0])
            oh1 = sb1("oh1", [P, CT, E0])
            oh2 = sb1("oh2", [P, CT, E0])
            tk = sb1("tk", [P, CT, E0])
            st = sb1("st", [P, 8, CT])
            score = sb1("score", [P, CT, E0])
            scoreT = sb1("scoreT", [E0, CS])
            h_bank = [ps[:, 0:2, :], ps[:, 2:4, :]]
            y_bank = [ps[:, 4, :], ps[:, 5, :]]
            ma, mb = ps[:, 6, :], ps[:, 7, :]
            s = l0
            block = ph.enter_context(nc.Block())

            def chunk(x, c, t=None):
                return x[:, bass.ds(c * CT, CT), :] if t is None else x[:, bass.ds(c * CT + t, 1), :].rearrange("p a d -> p (a d)")

            def over_chunks(eng, experts, ahead, sync):
                for i in range(2 * E0):
                    ahead(i, 0)
                sync(eng)
                with eng.Fori(0, CHUNKS - 1) as c:
                    for i in range(2 * E0):
                        experts(i, c)
                        ahead(i, c + 1)
                    experts(2 * E0, c)
                    sync(eng)
                for i in range(2 * E0 + 1):
                    experts(i, CHUNKS - 1)

            @block.sync
            def _(sp):
                for c in range(2):
                    lo, hi = (0, CT) if c == 0 else (CT, B * T)
                    sp.dma_start(x_all[:, lo:hi, :], a["x"].rearrange("b (t p) d -> p (b t) d", p=P)[:, lo:hi, :])\
                      .then_inc(x_loaded, DMA)

            @block.gpsimd
            def _(pool):
                steps = [0]

                def inverse_root(k, src, scale, eps):
                    steps[0] += 1
                    pool.tensor_scalar(var[:, k, :], src, scale, eps, ALU.mult, ALU.add).then_inc(s.pool_step, 1)
                    pool.wait_ge(s.pool_step, steps[0])
                    pool.tensor_tensor(rstd[:, k, :], var[:, k, :], half[:, 0:CT], ALU.pow).then_inc(s.rstd_ready, 1)

                def ahead(i, c):
                    if i == 0:
                        pool.wait_ge(s.ssq_ready, 1)
                        inverse_root(0, ssq[:, 0, :], 1.0 / D, RMS_EPS)
                    if i == 6:
                        pool.wait_ge(s.ssq_ready, 2)
                        inverse_root(1, ssq[:, 1, :], 1.0 / D, RMS_EPS)
                    if i == 13:
                        pool.wait_ge(s.lnvar_ready, 1)
                        inverse_root(2, mv[:, 0, :, 1], 1.0, LN_EPS)

                def experts(i, c):
                    if i == 2 * E0:
                        pool.wait_ge(s.acc_ready, 1)
                        inverse_root(3, mv[:, 1, :, 1], 1.0, LN_EPS)

                def sync(eng):
                    meet_and_clear(eng)
                    steps[0] = 0

                pool.memset(state[:, :, 0:1], 0.0)
                over_chunks(pool, experts, ahead, sync)

            @block.scalar
            def _(act):
                act.wait_ge(x_loaded, 2 * DMA)

                def ahead(i, c):
                    if i == 0:
                        for t in range(CT):
                            last = act.activation(junk[:, 0, t, :], chunk(x_all, c, t), ACT.Square,
                                                  accum_out=ssq[:, 0, t:t + 1])
                        last.then_inc(s.ssq_ready, 1)
                        act.wait_ge(s.xT_ps, 1)
                        act.copy(xT[:], ma).then_inc(s.xT_ready, 1)
                    if i == 1:
                        act.wait_ge(s.k_ps, 1)
                        act.copy(k_sb[:], ma).then_inc(s.k_sb_ready, 1)
                    if i == 2:
                        act.wait_ge(s.r_ps, 1)
                        act.activation(er[:], ma, ACT.Exp, scale=-1.0).then_inc(s.er_ready, 1)
                    if i == 6:
                        act.wait_ge(s.x1_ready, 1)
                        for t in range(CT):
                            last = act.activation(junk[:, 1, t, :], x1[:, t, :], ACT.Square, accum_out=ssq[:, 1, t:t + 1])
                        last.then_inc(s.ssq_ready, 1)
                    if i == 7:
                        act.wait_ge(s.xT_ps, 2)
                        act.copy(xT[:], ma).then_inc(s.xT_ready, 1)
                    if i in (8, 9, 10, 11):
                        f = i - 8
                        act.wait_ge(s.fc_ps, f + 1)
                        act.activation(z_half[:, f, :], (mb, ma)[f % 2], ACT.Copy, scale=0.5).then_inc(s.zhalf_ready, 1)
                    if i == 15:
                        act.wait_ge(s.xT_ps, 3)
                        act.copy(x3T[:], mb).then_inc(s.xT_ready, 1)

                def experts(i, c):
                    if i == 1:
                        act.wait_ge(s.lg_ready, 1)
                        act.activation(pr[:], lg[:], ACT.Exp).then_inc(s.pexp_ready, 1)
                    if i % 2 == 0 and i < 2 * E0:
                        e = i // 2
                        act.wait_ge(s.hmoe_ps, e + 1)
                        for k in range(HB):
                            last = act.activation(h_moe[:, e % 2, k, :], h_bank[e % 2][:, k, :], ACT.Relu,
                                                  bias=b1[:, e, k:k + 1])
                        last.then_inc(s.hmoe_ready, 1)
                    if i == 5:
                        act.wait_ge(s.scoreT_ps, 1)
                        act.copy(scoreT[:], mb[0:E0, :]).then_inc(s.scoreT_ready, 1)

                over_chunks(act, experts, ahead, meet)

            @block.vector
            def _(v):
                v.wait_ge(x_loaded, 2 * DMA)
                steps = [0]

                def link(ins):
                    steps[0] += 1
                    ins.then_inc(s.dve_step, 1)
                    v.wait_ge(s.dve_step, steps[0])

                def bn(k, src):
                    for t in range(CT):
                        last = v.bn_stats(bn6[:, k, t, :], src[:, t, :])
                    link(last)
                    for t in range(CT):
                        last = v.bn_aggr(mv[:, k, t, :], bn6[:, k, t, :])
                    return last

                def apply(k, src, dst):
                    for t in range(CT):
                        last = v.tensor_scalar(dst(t), src[:, t, :], mv[:, k, t, 0:1], rstd[:, 2 + k, t:t + 1],
                                               ALU.subtract, ALU.mult)
                    return last

                def ahead(i, c):
                    if i == 0:
                        v.wait_ge(s.rstd_ready, 1)
                        for t in range(CT):
                            last = v.tensor_scalar(xn[:, t, :], chunk(x_all, c, t), rstd[:, 0, t:t + 1], None, ALU.mult)
                        last.then_inc(s.xn_ready, 1)
                    if i == 1:
                        v.wait_ge(s.k_sb_ready, 1)
                        v.wait_ge(s.v_ps, 1)
                        v.tensor_tensor(kv[:], k_sb[:], mb, ALU.mult).then_inc(s.kv_ready, 1)
                        v.wait_ge(s.kv_ready, 1)
                        for n in range(CB):
                            last = v.tensor_tensor_scan(state[:, n, 1:S + 1], ew_bc[:], kv[:, n * S:(n + 1) * S], 0.0,
                                                        ALU.mult, ALU.add)
                        link(last)
                    if i == 2:
                        link(v.scalar_tensor_tensor(wkv[:].rearrange("p (n s) -> p n s", n=CB),
                                                    kv[:].rearrange("p (n s) -> p n s", n=CB), ew[:, 1:2],
                                                    state[:, :, 0:S], ALU.mult, ALU.add))
                        v.wait_ge(s.er_ready, 1)
                        link(v.tensor_scalar(gate[:], er[:], 1.0, None, ALU.add))
                        link(v.reciprocal(gate[:], gate[:]))
                        v.tensor_tensor(mixT[:], wkv[:], gate[:], ALU.mult).then_inc(s.mixT_ready, 1)
                    if i == 5:
                        v.wait_ge(s.mix_ps, 1)
                        msc = mixer_scale[:].unsqueeze(1).broadcast_to([P, CT, D])
                        link(v.tensor_tensor(tmp[:], tiles(ma, CT), msc, ALU.mult))
                        v.tensor_tensor(x1[:], tmp[:], chunk(x_all, c), ALU.add).then_inc(s.x1_ready, 1)
                    if i == 6:
                        v.wait_ge(s.rstd_ready, 2)
                        for t in range(CT):
                            last = v.tensor_scalar(xn[:, t, :], x1[:, t, :], rstd[:, 1, t:t + 1], None, ALU.mult)
                        last.then_inc(s.xn_ready, 1)
                    if i in (8, 9, 10, 11):
                        f = i - 8
                        v.wait_ge(s.zhalf_ready, f + 1)
                        v.tensor_tensor(h_fc[:, f, :], z_half[:, f, :], (mb, ma)[f % 2], ALU.max).then_inc(s.h_ready, 1)
                        v.wait_ge(s.h_ready, f + 1)
                        v.tensor_tensor(h_fc[:, f, :], h_fc[:, f, :], h_fc[:, f, :], ALU.mult).then_inc(s.hfc_ready, 1)
                    if i == 13:
                        v.wait_ge(s.mlp_ps, 1)
                        lsc = mlp_scale[:].unsqueeze(1).broadcast_to([P, CT, D])
                        link(v.tensor_tensor(tmp[:], tiles(ma, CT), lsc, ALU.mult))
                        link(v.tensor_tensor(tmp[:], tmp[:], x1[:], ALU.add))
                        link(v.tensor_tensor(tmp[:], tmp[:], chunk(x_all, c), ALU.add))
                        bn(0, tmp).then_inc(s.lnvar_ready, 1)
                        v.wait_ge(s.rstd_ready, 3)
                        apply(0, tmp, lambda t: x3[:, 0, t, :]).then_inc(s.xn_ready, 1)

                parts = softmax_top2(v, link, s, ma.rearrange("p (t x) -> p t x", t=CT)[:, :, 0:E0], E0, CT, None,
                                     lg[:], pr[:], tk[:], oh1[:], oh2[:], st, 1)

                def experts(i, c):
                    if i == 0:
                        link(v.tensor_copy(x3[:, 1], x3[:, 0]))
                        v.wait_ge(s.logit_ps, 1)
                        parts[0]()
                    if i == 1:
                        parts[1]()
                        parts[2]()
                        link(v.tensor_tensor(score[:], oh1[:], pr[:], ALU.mult))
                        link(v.reduce_sum(st[:, 6, :], score[:], AX))
                        link(v.reciprocal(st[:, 7, :], st[:, 6, :]))
                        v.tensor_tensor(score[:], score[:], st[:, 7, :].unsqueeze(2).broadcast_to([P, CT, E0]),
                                        ALU.mult).then_inc(s.score_ready, 1)
                        v.wait_ge(s.score_ready, 1)
                    if i >= 3 and i % 2 == 1 or i == 2 * E0:
                        for e in ([0] if i == 3 else [(i - 3) // 2] if i < 2 * E0 else [E0 - 1]):
                            v.wait_ge(s.ymoe_ps, e + 1)
                            for t in range(CT):
                                last = v.scalar_tensor_tensor(acc[:, t, :], y_bank[e % 2][:, t * D:(t + 1) * D],
                                                              score[:, t, e:e + 1], (x3[:, 1] if e == 0 else acc)[:, t, :],
                                                              ALU.mult, ALU.add)
                            last.then_inc(s.ymoe_used, 1)
                            v.wait_ge(s.ymoe_used, e + 1)
                    if i == 7:
                        v.wait_ge(s.acc0_ps, 1)
                        v.tensor_tensor(acc[:], acc[:], tiles(mb, CT), ALU.add).then_inc(s.acc0_used, 1)
                        v.wait_ge(s.acc0_used, 1)
                    if i == 2 * E0:
                        bn(1, acc).then_inc(s.acc_ready, 1)
                        v.wait_ge(s.rstd_ready, 4 if ahead_too[0] else 1)
                        link(apply(1, acc, lambda t: chunk(x4_all, c, t)))

                def sync(eng):
                    meet(eng)
                    steps[0] = 0

                ahead_too = [True]

                def last_too(i, c):
                    ahead_too[0] = not isinstance(c, int)
                    experts(i, c)

                over_chunks(v, last_too, ahead, sync)

            @block.tensor
            def _(pe):
                def mm(o, l, r, start=True, stop=True):
                    return pe.matmul(o, l, r, start=start, stop=stop)

                def transposes(dst, src):
                    for t in range(CT):
                        last = pe.transpose(dst[:, t * P:(t + 1) * P], src[:, t, :], ident[:])
                    return last

                def ahead(i, c):
                    if i == 0:
                        pe.wait_ge(s.xn_ready, 1)
                        transposes(ma, xn).then_inc(s.xT_ps, 1)
                    if i == 1:
                        pe.wait_ge(s.xT_ready, 1)
                        mm(ma, wkvr[:, 0, :], xT[:]).then_inc(s.k_ps, 1)
                        mm(mb, wkvr[:, 1, :], xT[:]).then_inc(s.v_ps, 1)
                    if i == 2:
                        pe.wait_ge(s.k_sb_ready, 1)
                        mm(ma, wkvr[:, 2, :], xT[:]).then_inc(s.r_ps, 1)
                    if i == 5:
                        pe.wait_ge(s.mixT_ready, 1)
                        for t in range(CT):
                            last = mm(ma[:, t * D:(t + 1) * D], mixT[:, t * P:(t + 1) * P], wo0[:])
                        last.then_inc(s.mix_ps, 1)
                    if i == 7:
                        pe.wait_ge(s.xn_ready, 2)
                        transposes(ma, xn).then_inc(s.xT_ps, 1)
                    if i in (8, 9, 10, 11):
                        f = i - 8
                        if f == 0:
                            pe.wait_ge(s.xT_ready, 2)
                            if not isinstance(c, int):
                                pe.wait_ge(s.acc0_used, 1)
                        if f >= 2:
                            pe.wait_ge(s.h_ready, f - 1)
                        mm((mb, ma)[f % 2], wfc[:, f * P:(f + 1) * P], xT[:]).then_inc(s.fc_ps, 1)
                    if i == 12:
                        pe.wait_ge(s.hfc_ready, FC)
                        for t in range(CT):
                            for f in range(FC):
                                last = mm(ma[:, t * D:(t + 1) * D], h_fc[:, f, t * P:(t + 1) * P], wmlp[:, f, :],
                                          start=f == 0, stop=f == FC - 1)
                        last.then_inc(s.mlp_ps, 1)
                    if i == 15:
                        pe.wait_ge(s.xn_ready, 3)
                        transposes(mb, x3[:, 0]).then_inc(s.xT_ps, 1)

                def experts(i, c):
                    if i == 0:
                        for t in range(CT):
                            last = mm(ma[:, t * P:t * P + E0], x3T[:, t * P:(t + 1) * P], wg[:])
                        last.then_inc(s.logit_ps, 1)
                        hidden(0)
                        pe.wait_ge(s.lg_ready, 1)
                    if i % 2 == 0 and i // 2 + 1 < E0:
                        hidden(i // 2 + 1)
                    if i == 4:
                        pe.wait_ge(s.score_ready, 1)
                        if not isinstance(c, int):
                            pe.wait_ge(s.kv_ready, 1)
                        for t in range(CT):
                            last = pe.transpose(mb[0:E0, t * P:(t + 1) * P], score[:, t, :], ident[:])
                        last.then_inc(s.scoreT_ps, 1)
                    if i == 6:
                        pe.wait_ge(s.scoreT_ready, 1)
                        for t in range(CT):
                            last = mm(mb[:, t * D:(t + 1) * D], scoreT[:, t * P:(t + 1) * P], b2[:])
                        last.then_inc(s.acc0_ps, 1)
                    if i % 2 == 1:
                        e = i // 2
                        pe.wait_ge(s.hmoe_ready, e + 1)
                        if e >= 2:
                            pe.wait_ge(s.ymoe_used, e - 1)
                        for t in range(CT):
                            for k in range(HB):
                                last = mm(y_bank[e % 2][:, t * D:(t + 1) * D], h_moe[:, e % 2, k, t * P:(t + 1) * P],
                                          w2[:, e, k, :], start=k == 0, stop=k == HB - 1)
                        last.then_inc(s.ymoe_ps, 1)

                def hidden(e):
                    if e >= 2:
                        pe.wait_ge(s.hmoe_ready, e - 1)
                    for k in range(HB):
                        last = mm(h_bank[e % 2][:, k, :], w1[:, e, k * P:(k + 1) * P], x3T[:])
                    last.then_inc(s.hmoe_ps, 1)

                over_chunks(pe, experts, ahead, meet)

        def unit(group, u):
            return Unit(sets[group % 2], u, u if group < B - 1 else u - 1, group % 2)

        def norms_of(unit):
            return 1 if unit.u == 0 or unit.n < unit.u else 2

        def units(group):
            return [unit(group, u) if (u == 0 and group < B - 1) or (u > 0 and group >= 0) else None for u in range(U)]

        def over_units(eng, period):
            def group(g, n, chain):
                seq = [units(g - 1)[-1]] + units(g) + (units(g + 1) if g + 1 < B else [None] * U)
                for p in range(U):
                    period(p, g, n, chain, seq[p:p + 5])

            for p in (2, 3, 4):
                seq = [None] * (U + 1) + units(-1)
                period(p, -2, -2, 0, seq[p:p + 5])
            group(-1, -1, 1)
            group(0, 0, 0)
            with eng.Fori(0, (B - 4) // 2) as r:
                group(1, r * 2 + 1, 1)
                group(2, r * 2 + 2, 0)
            for g in range(B - 3, B):
                group(g, g, g % 2)
            period(0, B, B, 0, [unit(B - 1, U - 1), None, None, None, None])

        with ExitStack() as ph:
            def sb2(name, shape, dt=F32):
                return ph.enter_context(nc.sbuf_tensor(name, shape, dt))

            x4 = sb2("x4", [P, T, D])
            x4T = sb2("x4T", [D, S])
            x5 = sb2("x5", [P, T, D])
            x5T = sb2("x5T", [D, S])
            x5_sum = sb2("x5_sum", [P, T, D])
            acc = sb2("acc2", [P, 2, T, D])
            y = sb2("y", [P, 2, T, D])
            bn6 = sb2("bn6_2", [P, T, 6])
            mv = sb2("mv_2", [P, 2, T, 2])
            var = sb2("var_2", [P, 2, T])
            rstd = sb2("rstd_2", [P, 2, T])
            lg = sb2("lg_2", [P, T, E1])
            pr = sb2("pr_2", [P, T, E1])
            oh1 = sb2("oh1_2", [P, T, E1])
            oh2 = sb2("oh2_2", [P, T, E1])
            tk = sb2("tk_2", [P, T, E1])
            st = sb2("st_2", [P, 8, T])
            key_mask = sb2("key_mask", [P, 2, T, E1])
            w_tok = sb2("w_tok", [P, 2, T, E1])
            scoreT = sb2("scoreT_2", [E1, S])
            qkv = sb2("qkv", [P, 3, T, D])
            sq = sb2("sq", [P, 2, T, D])
            ms = sb2("ms", [P, 2 * T * H])
            rqk = sb2("rqk", [P, 2 * T * H])
            q_split = sb2("q_split", [P, T, H, SLOT], F16)
            k_split = sb2("k_split", [P, T, H, SLOT], F16)
            v_ext = sb2("v_ext", [P, U, T, H, SLOT])
            qT = sb2("qT", [P, G, S], F16)
            kT = sb2("kT", [P, U, G, S], F16)
            q_diag = sb2("q_diag", [P, U, J, G, S], F16)
            mx = sb2("mx", [P, U, T, H])
            mneg = sb2("mneg", [P, U, T, H], F16)
            mT = sb2("mT", [H, U, S], F16)
            PB = 4
            probs = sb2("probs", [P, PB, J, S])
            oT = sb2("oT", [P, G, S])
            rden = sb2("rden", [P, T, H])
            y_n = sb2("y_n", [P, T, D])
            yT = sb2("yT", [D, S])

            def s_bank(i):
                return ps[:, i % 2, :]

            def max_bank(i):
                return ps[:, 2 + i % 2, :]

            def o_bank(i):
                return ps[:, 4 + i, :]

            m0, m1 = ps[:, 6, :], ps[:, 7, :]
            both = ps[:, 6:8, :]

            with nc.Block() as block:
                @block.gpsimd
                def _(pool):
                    for i, x in enumerate((q_diag, q_split, k_split, v_ext)):
                        pool.memset(x[:], 0.0).then_inc(const_ready, 1)
                    pool.wait_ge(const_ready, CONSTS + 4)
                    pool.memset(q_split[:, :, :, MASK_ROW:MASK_ROW + 1], 1.0)
                    pool.memset(k_split[:, :, :, SHIFT_ROW:SHIFT_ROW + 1], 1.0)
                    for u in range(U):
                        last = pool.memset(v_ext[:, u, :, :, HD:HD + 1], 1.0)
                    last.then_inc(const_ready, 1)
                    pool.wait_ge(const_ready, CONSTS + 5)

            block = ph.enter_context(nc.Block())

            def hand_back(eng, p, g):
                if p == 1 and g >= -1:
                    eng.drain().then_inc(done[(g - 1) % 2], 1)

            def await_clean(eng, p, g):
                if p == 2 and g >= -1:
                    eng.wait_ge(clean[(g + 1) % 2], 1)
                    eng.drain()

            def half_of(i, nxt, nxt2):
                return (nxt, i + LEAD) if i + LEAD < HALVES else (nxt2, i + LEAD - HALVES)

            @block.sync
            def _(sp):
                def period(p, g, n, chain, k):
                    prev, cur, nxt, nxt2, nxt3 = k
                    hand_back(sp, p, g)
                    if nxt2:
                        sp.wait_ge(nxt2.s.qT_ready, nxt2.n + 1)
                        for j in range(J):
                            sp.dma_start(q_diag[SLOT * j:SLOT * (j + 1), nxt2.u, j, :, :],
                                         qT[SLOT * j:SLOT * (j + 1), :, :]).then_inc(nxt2.s.diag_ready, DMA)
                    if nxt:
                        sp.wait_ge(nxt.s.mT_ready, nxt.n + 1)
                        for j in range(J):
                            row = SLOT * j + SHIFT_ROW
                            sp.dma_start(q_diag[row:row + 1, nxt.u, j, :, :], mT[j:H:J, nxt.u, :])\
                              .then_inc(nxt.s.shift_ready, DMA)
                    await_clean(sp, p, g)
                    if prev and p == 0:
                        sp.wait_ge(prev.s.y_ready, 1)
                        sp.dma_start(out[bass.ds(n - 1, 1), :, :].rearrange("b (t p) d -> p (b t) d", p=P),
                                     y[:, prev.parity]).then_inc(stored, DMA)

                over_units(sp, period)
                sp.wait_ge(stored, DMA * B)

            @block.gpsimd
            def _(pool):
                steps = {0: 0, 1: 0}

                def link(ins, chain):
                    steps[chain] += 1
                    ins.then_inc(sets[chain].pool_step, 1)
                    pool.wait_ge(sets[chain].pool_step, steps[chain])

                def part(x, c):
                    return x[:].rearrange("p t h s -> p (t h) s")[:, :, c * HD:(c + 1) * HD]

                def split(unit, chain):
                    qf = qkv[:, 0].rearrange("p t (h d) -> p (t h) d", h=H)
                    kf = qkv[:, 1].rearrange("p t (h d) -> p (t h) d", h=H)
                    pool.tensor_copy(part(k_split, 0), kf)
                    link(pool.tensor_copy(part(q_split, 0), qf), chain)
                    pool.tensor_tensor(part(k_split, 1), kf, part(k_split, 0), ALU.subtract)
                    pool.tensor_copy(part(k_split, 2), part(k_split, 0))
                    pool.tensor_tensor(part(q_split, 2), qf, part(q_split, 0), ALU.subtract)
                    if unit.u == 0:
                        pool.memset(k_split[:, :, :, MASK_ROW:MASK_ROW + 1], 0.0)
                    else:
                        for t in range(T):
                            pool.tensor_copy(k_split[:, t, :, MASK_ROW:MASK_ROW + 1],
                                             key_mask[:, unit.parity, t, unit.u - 1:unit.u].unsqueeze(1).broadcast_to([P, H, 1]))
                    pool.tensor_copy(part(q_split, 1), part(q_split, 0)).then_inc(unit.s.split_ready, 1)

                def inverse_root(unit, k):
                    link(pool.tensor_scalar(var[:, k, :], mv[:, k, :, 1], 1.0, LN_EPS, ALU.mult, ALU.add), unit.parity)
                    pool.tensor_tensor(rstd[:, k, :], var[:, k, :], half[:, 0:T], ALU.pow).then_inc(unit.s.rstd_ready, 1)

                def period(p, g, n, chain, k):
                    prev, cur, nxt, nxt2, nxt3 = k
                    hand_back(pool, p, g)
                    if p == 2 and g >= -1:
                        q = (g - 1) % 2
                        pool.wait_ge(done[q], 5)
                        pool.sem_clear(sets[q].numbers)
                        pool.sem_clear(done[q])
                        pool.sem_clear(clean[1 - q])
                        pool.sem_inc(clean[q], 1)
                        steps[q] = 0
                        await_clean(pool, p, g)
                    if p == 2 and nxt3:
                        if g >= -1:
                            pool.wait_ge(sets[g % 2].x4_used, 1)
                        pool.tensor_copy(x4[:], x4_all[:, bass.ds((n + 2) * T, T), :]).then_inc(nxt3.s.x4_ready, 1)
                    if nxt2 and nxt2.u == 0:
                        pool.wait_ge(nxt2.s.qn_ready, 1)
                        split(nxt2, chain)
                    if prev and prev.u in (0, U - 1):
                        pool.wait_ge(prev.s.lnvar_ready, norms_of(prev))
                        inverse_root(prev, 0 if prev.u == 0 else 1)
                    if nxt3:
                        pool.wait_ge(nxt3.s.qkv_ready, nxt3.n + 1)
                        pool.tensor_copy(v_ext[:, nxt3.u, :, :, 0:HD],
                                         qkv[:, 2].rearrange("p t (h d) -> p t h d", h=H)).then_inc(nxt3.s.v_ready, 1)
                        if nxt3.u == 0:
                            pool.wait_ge(nxt3.s.qkms_ready, 1)
                            link(pool.tensor_scalar(ms[:], ms[:], 1.0 / HD, RMS_EPS, ALU.mult, ALU.add), nxt3.parity)
                            pool.tensor_tensor(rqk[:], ms[:], half[:], ALU.pow).then_inc(nxt3.s.rqk_ready, 1)
                        else:
                            if nxt3.u == 1:
                                pool.wait_ge(sets[1 - nxt3.parity].route_ready, 1)
                            split(nxt3, chain)

                over_units(pool, period)

            @block.scalar
            def _(act):
                def period(p, g, n, chain, k):
                    prev, cur, nxt, nxt2, nxt3 = k
                    hand_back(act, p, g)
                    for i in range(HALVES):
                        if cur:
                            act.wait_ge(cur.s.s_ps, cur.n * HALVES + i + 1)
                            act.activation(probs[:, (i // 2) % PB, 2 * (i % 2):2 * (i % 2) + 2, :].rearrange("p j s -> p (j s)"),
                                           s_bank(i), ACT.Exp, scale=HD ** -0.5 if cur.u == 0 else 0.5)\
                               .then_inc(cur.s.probs_ready, 1)
                        if i == 1 and p == 2 and -1 <= g < B - 1:
                            act.wait_ge(sets[g % 2].x5T_ps, 1)
                            act.copy(x5T[:], m0[:, 0:S]).then_inc(sets[g % 2].x5T_ready, 1)
                        if i == 1 and p == 3 and g >= -1 and g < B - 1:
                            act.wait_ge(sets[g % 2].scoreT_ps, 1)
                            act.copy(scoreT[:], m0[0:E1, 0:S]).then_inc(sets[g % 2].scoreT_ready, 1)
                        if i == 2 and prev:
                            act.wait_ge(prev.s.pv_done, prev.n * (HALVES // 2) + HALVES // 2)
                            act.copy(oT[:, 2:4, :].rearrange("p g s -> p (g s)"), o_bank(1)).then_inc(prev.s.oT_ready, 1)
                        if i == 5 and prev:
                            act.wait_ge(prev.s.yT_ps, prev.n + 1)
                            act.copy(yT[:], m0[:, 0:S]).then_inc(prev.s.yT_ready, 1)
                        if i == 8 and nxt2:
                            act.wait_ge(nxt2.s.tq_ps, nxt2.n + 1)
                            act.copy(qT[:].rearrange("p g s -> p (g s)"), m1.bitcast(F16)[:, 0:G * S])\
                               .then_inc(nxt2.s.qT_ready, 1)
                        if i == 8 and p == 2 and g >= -1 and g < B - 1:
                            act.wait_ge(sets[g % 2].lg_ready, 1)
                            act.activation(pr[:], lg[:], ACT.Exp).then_inc(sets[g % 2].pexp_ready, 1)
                        if i == 10 and cur:
                            act.wait_ge(cur.s.pv_done, cur.n * (HALVES // 2) + HALVES // 4)
                            act.copy(oT[:, 0:2, :].rearrange("p g s -> p (g s)"), o_bank(0)).then_inc(cur.s.oT_ready, 1)
                        if i == 11 and p == 2:
                            await_clean(act, p, g)
                            if nxt3:
                                act.wait_ge(nxt3.s.x4T_ps, 1)
                                act.copy(x4T[:], m0[:, 0:S]).then_inc(nxt3.s.x4T_ready, 1)
                        if i == 12 and nxt:
                            act.wait_ge(nxt.s.mT_ps, nxt.n + 1)
                            act.copy(mT[:, nxt.u], m0.bitcast(F16)[0:H, 0:S]).then_inc(nxt.s.mT_ready, 1)

                over_units(act, period)

            @block.vector
            def _(v):
                steps = {0: 0, 1: 0}
                now = [0]

                def link(ins):
                    chain = now[0]
                    steps[chain] += 1
                    ins.then_inc(sets[chain].dve_step, 1)
                    v.wait_ge(sets[chain].dve_step, steps[chain])

                def layer_norm(unit, k, src, dst, dst_sem):
                    for t in range(T):
                        last = v.bn_stats(bn6[:, t, :], src[:, t, :])
                    link(last)
                    for t in range(T):
                        last = v.bn_aggr(mv[:, k, t, :], bn6[:, t, :])
                    last.then_inc(unit.s.lnvar_ready, 1)
                    yield
                    v.wait_ge(unit.s.rstd_ready, norms_of(unit))
                    for t in range(T):
                        last = v.tensor_scalar(dst[:, t, :], src[:, t, :], mv[:, k, t, 0:1], rstd[:, k, t:t + 1],
                                               ALU.subtract, ALU.mult)
                    last.then_inc(dst_sem, 1)
                    yield

                def period(p, g, n, chain, k):
                    prev, cur, nxt, nxt2, nxt3 = k
                    if p == 0:
                        steps[chain] = 0
                    now[0] = chain
                    hand_back(v, p, g)
                    own = sets[g % 2]
                    routing = p in (2, 3) and -1 <= g < B - 1
                    if routing:
                        parts = softmax_top2(v, link, own, m1.rearrange("p (t x) -> p t x", t=T)[:, :, 0:E1], E1, T,
                                             router_b, lg[:], pr[:], tk[:], oh1[:], oh2[:], st, 1)
                    if nxt2 and nxt2.u == 0:
                        v.wait_ge(nxt2.s.rqk_ready, 1)
                        qk = qkv[:, 0:2].rearrange("p c t (h d) -> p (c t h) d", h=H)
                        link(v.tensor_tensor(qk, qk, rqk[:].unsqueeze(2).broadcast_to([P, 2 * T * H, HD]), ALU.mult))
                        for c in range(2):
                            qc = qkv[:, c].rearrange("p t (h d) -> p (t h) d", h=H)
                            last = v.tensor_tensor(qc, qc, qk_w[:, c, :].unsqueeze(1).broadcast_to([P, T * H, HD]), ALU.mult)
                        last.then_inc(nxt2.s.qn_ready, 1)
                    for i in range(HALVES):
                        unit, m = half_of(i, nxt, nxt2)
                        if unit:
                            t, g_, jp = m // (2 * G), m // 2 % G, m % 2
                            v.wait_ge(unit.s.smax_ps, unit.n * HALVES + m + 1)
                            v.reduce_max(mx[:, unit.u, t, J * g_ + 2 * jp:J * g_ + 2 * jp + 2],
                                         max_bank(m).rearrange("p (c k) -> p c k", c=2), AX).then_inc(unit.s.smax_used, 1)
                        if i == HALVES - 1 - LEAD and nxt:
                            v.wait_ge(nxt.s.smax_used, (nxt.n + 1) * HALVES)
                            v.tensor_scalar(mneg[:, nxt.u], mx[:, nxt.u], -1.0, None, ALU.mult).then_inc(nxt.s.mneg_ready, 1)
                        if i == 4 and prev:
                            v.wait_ge(prev.s.oN_ps, prev.n + 1)
                            oN = both.rearrange("p t (h s) -> p t h s", h=H)
                            link(v.reciprocal(rden[:], oN[:, :, :, HD]))
                            if prev.u > 0:
                                link(v.tensor_tensor(rden[:], rden[:], w_tok[:, prev.parity, :, prev.u - 1].unsqueeze(2)
                                                     .broadcast_to([P, T, H]), ALU.mult))
                            v.tensor_tensor(y_n[:].rearrange("p t (h d) -> p (t h) d", h=H),
                                            both.rearrange("p t (h s) -> p (t h) s", h=H)[:, :, 0:HD],
                                            rden[:].rearrange("p t h -> p (t h)").unsqueeze(2).broadcast_to([P, T * H, HD]),
                                            ALU.mult).then_inc(prev.s.yn_ready, 1)
                        if i == 6 and routing and p == 2:
                            v.wait_ge(own.logit_ps, 1)
                            parts[0]()
                        if i == 7 and p == 3 and routing:
                            v.wait_ge(own.acc0_ps, 1)
                            v.tensor_tensor(acc[:, 1 - g % 2], tiles(m1[:, 0:T * D]), x5[:], ALU.add).then_inc(own.acc0_used, 1)
                        if i == 8 and nxt2:
                            v.wait_ge(nxt2.s.tk_ps, nxt2.n + 1)
                            v.tensor_copy(kT[:, nxt2.u].rearrange("p g s -> p (g s)"), m0.bitcast(F16)[:, 0:G * S])\
                             .then_inc(nxt2.s.kT_ready, 1)
                        if i == 10 and routing and p == 2:
                            parts[1]()
                        if i == 12 and routing and p == 2:
                            parts[2]()
                            link(v.tensor_scalar(key_mask[:, 1 - g % 2], oh1[:], -MASKED, MASKED, ALU.mult, ALU.add))
                            v.tensor_tensor(w_tok[:, 1 - g % 2], oh1[:], pr[:], ALU.mult).then_inc(own.route_ready, 1)
                        if i == 10 and prev:
                            v.wait_ge(prev.s.proj_ps, prev.n + 1)
                            pj = tiles(m1[:, 0:T * D])
                            if prev.u == 0:
                                v.tensor_tensor(x5_sum[:], pj, bproj[:].unsqueeze(1).broadcast_to([P, T, D]),
                                                ALU.add).then_inc(prev.s.proj_used, 1)
                                v.wait_ge(prev.s.proj_used, prev.n + 1)
                                v.tensor_tensor(x5_sum[:], x5_sum[:], x4[:], ALU.add).then_inc(prev.s.x4_used, 1)
                                v.wait_ge(prev.s.x4_used, 1)
                                norm = layer_norm(prev, 0, x5_sum, x5, prev.s.x5_ready)
                            else:
                                a_ = acc[:, prev.parity]
                                v.tensor_tensor(a_, a_, pj, ALU.add).then_inc(prev.s.proj_used, 1)
                                if prev.u == U - 1:
                                    v.wait_ge(prev.s.proj_used, prev.n + 1)
                                    norm = layer_norm(prev, 1, a_, y[:, prev.parity], prev.s.y_ready)
                            if prev.u in (0, U - 1):
                                next(norm)
                        if i == 13 and prev and prev.u in (0, U - 1):
                            next(norm)
                        if i == 13:
                            await_clean(v, p, g)
                        if i == 14 and nxt3:
                            v.wait_ge(nxt3.s.qkv_ps, nxt3.n + 1)
                            for t in range(T):
                                last = v.tensor_tensor(qkv[:, :, t, :], both[:, t, 0:3 * D].rearrange("p (c d) -> p c d", c=3),
                                                       bqkv[:, nxt3.u, :].rearrange("p (c d) -> p c d", c=3), ALU.add)
                            last.then_inc(nxt3.s.qkv_ready, 1)
                            if nxt3.u == 0:
                                v.wait_ge(nxt3.s.qkv_ready, 1)
                                link(v.tensor_tensor(sq[:], qkv[:, 0:2], qkv[:, 0:2], ALU.mult))
                                v.reduce_sum(ms[:], sq[:].rearrange("p c t (h d) -> p (c t h) d", h=H), AX)\
                                 .then_inc(nxt3.s.qkms_ready, 1)

                over_units(v, period)

            @block.tensor
            def _(pe):
                def mm(o, l, r, start=True, stop=True):
                    return pe.matmul(o, l, r, start=start, stop=stop)

                def scores(unit, i, before):
                    g, t, jp = i // 4, i // 2 % T, i % 2
                    if i == 0:
                        pe.wait_ge(unit.s.shift_ready, (unit.n + 1) * (DMA * J))
                    if i >= 2:
                        pe.wait_ge(unit.s.probs_ready, unit.n * HALVES + i - 1)
                    elif before:
                        pe.wait_ge(before.s.probs_ready, before.n * HALVES + HALVES - 1 + i)
                    mm(s_bank(i), kT[:, unit.u, g, t * P:(t + 1) * P], q_diag[:, unit.u, 2 * jp:2 * jp + 2, g, :])\
                        .then_inc(unit.s.s_ps, 1)

                def weigh(unit, i):
                    g, t = i // T, i % T
                    pe.wait_ge(unit.s.probs_ready, unit.n * HALVES + 2 * i + 2)
                    if i == 0:
                        pe.wait_ge(unit.s.v_ready, unit.n + 1)
                    for j in range(J):
                        last = mm(o_bank(g // 2)[SLOT * j:SLOT * (j + 1), (g % 2) * S:(g % 2 + 1) * S],
                                  v_ext[:, unit.u, t, J * g + j, :], probs[:, i % PB, j, :], start=t == 0, stop=t == T - 1)
                    last.then_inc(unit.s.pv_done, 1)

                def max_scores(unit, m, before):
                    t, g, jp = m // (2 * G), m // 2 % G, m % 2
                    if m == 0:
                        pe.wait_ge(unit.s.diag_ready, (unit.n + 1) * (DMA * J))
                        pe.wait_ge(unit.s.kT_ready, unit.n + 1)
                    if m >= 2:
                        pe.wait_ge(unit.s.smax_used, unit.n * HALVES + m - 1)
                    elif before:
                        pe.wait_ge(before.s.smax_used, before.n * HALVES + HALVES - 1 + m)
                    for j in range(2):
                        last = mm(max_bank(m)[:, j * S:(j + 1) * S], q_diag[:, unit.u, 2 * jp + j, g, t * P:(t + 1) * P],
                                  kT[:, unit.u, g, :])
                    last.then_inc(unit.s.smax_ps, 1)

                def period(p, g, n, chain, k):
                    prev, cur, nxt, nxt2, nxt3 = k
                    own = sets[g % 2]
                    hand_back(pe, p, g)
                    routing = -1 <= g < B - 1
                    for i in range(HALVES):
                        if i + 1 < HALVES and cur:
                            scores(cur, i + 1, prev)
                        unit, m = half_of(i, nxt, nxt2)
                        if unit:
                            max_scores(unit, m, nxt if unit is nxt2 else None)
                        if i == 1 and prev:
                            weigh(prev, HALVES // 2 - 1)
                        if i >= 3 and i % 2 == 1 and cur:
                            if i in (3, 11) and prev:
                                pe.wait_ge(prev.s.oT_ready, 2 * prev.n + (1 if i == 3 else 2))
                            weigh(cur, (i - 3) // 2)
                        if i == 1 and p in (2, 3) and routing:
                            if nxt2:
                                pe.wait_ge(nxt2.s.qkv_ready, nxt2.n + 1)
                            if p == 2:
                                pe.wait_ge(own.x5_ready, 1)
                                for t in range(T):
                                    last = pe.transpose(m0[:, t * P:(t + 1) * P], x5[:, t, :], ident[:])
                                last.then_inc(own.x5T_ps, 1)
                            else:
                                pe.wait_ge(own.route_ready, 1)
                                for t in range(T):
                                    last = pe.transpose(m0[0:E1, t * P:(t + 1) * P], w_tok[:, 1 - g % 2, t, :], ident[:])
                                last.then_inc(own.scoreT_ps, 1)
                        if i == 3:
                            if nxt2:
                                pe.wait_ge(nxt2.s.qkv_ready, nxt2.n + 1)
                            if p == 2 and routing:
                                pe.wait_ge(own.x5T_ready, 1)
                            if p == 3 and routing:
                                pe.wait_ge(own.scoreT_ready, 1)
                            if prev:
                                pe.wait_ge(prev.s.oT_ready, 2 * prev.n + 2)
                                for t in range(T):
                                    for g_ in range(G):
                                        last = pe.transpose(both[:, t, g_ * P:(g_ + 1) * P], oT[:, g_, t * P:(t + 1) * P], ident[:])
                                last.then_inc(prev.s.oN_ps, 1)
                        if i == 5 and prev:
                            pe.wait_ge(prev.s.yn_ready, prev.n + 1)
                            for t in range(T):
                                last = pe.transpose(m0[:, t * P:(t + 1) * P], y_n[:, t, :], ident[:])
                            last.then_inc(prev.s.yT_ps, 1)
                        if i == 6 and routing and p == 2:
                            for t in range(T):
                                last = mm(m1[:, t * S:t * S + E1], x5T[:, t * P:(t + 1) * P], router_w[:])
                            last.then_inc(own.logit_ps, 1)
                        if i == 6 and routing and p == 3:
                            for t in range(T):
                                last = mm(m1[:, t * D:(t + 1) * D], scoreT[:, t * P:(t + 1) * P], bo[:])
                            last.then_inc(own.acc0_ps, 1)
                        if i == 7:
                            if prev:
                                pe.wait_ge(prev.s.yT_ready, prev.n + 1)
                            if p == 2 and routing:
                                pe.wait_ge(own.lg_ready, 1)
                            if p == 3 and routing:
                                pe.wait_ge(own.acc0_used, 1)
                            if nxt2:
                                pe.wait_ge(nxt2.s.split_ready, nxt2.n + 1)
                                for dst, src, ready in ((m0, k_split, nxt2.s.tk_ps), (m1, q_split, nxt2.s.tq_ps)):
                                    for g_ in range(G):
                                        for t in range(T):
                                            last = pe.transpose(dst.bitcast(F16)[:, g_ * S + t * P:g_ * S + (t + 1) * P],
                                                                src[:, t, J * g_:J * (g_ + 1), :].rearrange("p h s -> p (h s)"),
                                                                ident16[:])
                                    last.then_inc(ready, 1)
                        if i == 9:
                            if nxt2:
                                pe.wait_ge(nxt2.s.qT_ready, nxt2.n + 1)
                                pe.wait_ge(nxt2.s.kT_ready, nxt2.n + 1)
                            if prev:
                                for t in range(T):
                                    last = mm(m1[:, t * D:(t + 1) * D], yT[:, t * P:(t + 1) * P], wproj[:, prev.u, :])
                                last.then_inc(prev.s.proj_ps, 1)
                        if i == 10 and p == 2:
                            await_clean(pe, p, g)
                            if nxt3:
                                pe.wait_ge(nxt3.s.x4_ready, 1)
                                for t in range(T):
                                    last = pe.transpose(m0[:, t * P:(t + 1) * P], x4[:, t, :], ident[:])
                                last.then_inc(nxt3.s.x4T_ps, 1)
                        if i == 11:
                            if p == 2 and nxt3:
                                pe.wait_ge(nxt3.s.x4T_ready, 1)
                            if nxt:
                                pe.wait_ge(nxt.s.mneg_ready, nxt.n + 1)
                                for t in range(T):
                                    last = pe.transpose(m0.bitcast(F16)[0:H, t * P:(t + 1) * P], mneg[:, nxt.u, t, :], ident16[:])
                                last.then_inc(nxt.s.mT_ps, 1)
                        if i == 13 and nxt:
                            pe.wait_ge(nxt.s.mT_ready, nxt.n + 1)
                        if i == 13 and prev:
                            pe.wait_ge(prev.s.proj_used, prev.n + 1)
                        if i == 13 and nxt3:
                            src = x4T if nxt3.u == 0 else x5T
                            for t in range(T):
                                last = mm(both[:, t, 0:3 * D], src[:, t * P:(t + 1) * P], wqkv[:, nxt3.u, :])
                            last.then_inc(nxt3.s.qkv_ps, 1)
                        if i == HALVES - 1 and nxt:
                            scores(nxt, 0, cur)

                over_units(pe, period)


def kernel(**inputs):
    import concourse.bacc as bacc
    from concourse.bass_utils import run_bass_kernel_spmd

    f = {k: np.ascontiguousarray(v) for k, v in inputs.items()}
    c = np.ascontiguousarray
    a = {
        "x": f["L0_attn_x"],
        "wkvr": c(np.stack([f["L0_attn_Wk"].T, f["L0_attn_Wv"].T, f["L0_attn_Wr"].T])),
        "wo0": c(f["L0_attn_Wo"].T),
        "decay": c(np.stack([f["L0_attn_time_decay"], f["L0_attn_time_first"]], axis=1)),
        "mixer_scale": f["L0_attn_mixer_scale"],
        "wfc": c(f["L0_attn_Wfc"].T),
        "wmlp": c(f["L0_attn_Wmlp"].T),
        "mlp_scale": f["L0_attn_mlp_scale"],
        "wg": f["L0_ffn_Wg"], "w1": f["L0_ffn_W1"], "b1": f["L0_ffn_b1"], "w2": f["L0_ffn_W2"], "b2": f["L0_ffn_b2"],
        "wqkv": c(np.concatenate([f["L1_attn_W_qkv"][None],
                                  np.concatenate([f["L1_ffn_wq"], f["L1_ffn_wk"], f["L1_ffn_wv"]], axis=2)])),
        "bqkv": c(np.concatenate([f["L1_attn_b_qkv"][None],
                                  np.concatenate([f["L1_ffn_bq"], f["L1_ffn_bk"], f["L1_ffn_bv"]], axis=1)])),
        "wproj": c(np.concatenate([f["L1_attn_W_proj"][None], f["L1_ffn_wo"]])),
        "bproj": f["L1_attn_b_proj"],
        "bo": f["L1_ffn_bo"],
        "qk_w": c(np.stack([f["L1_attn_qn_w"], f["L1_attn_kn_w"]])),
        "router_w": f["L1_ffn_router_w"], "router_b": f["L1_ffn_router_b"],
    }
    nc = bacc.Bacc("TRN2", target_bir_lowering=False, num_devices=1)
    aps = {k: nc.dram_tensor("in_" + k, v.shape, F32, kind="ExternalInput").ap() for k, v in a.items()}
    out = nc.dram_tensor("out_0", (B, S, D), F32, kind="ExternalOutput").ap()
    program(nc, aps, out)
    r = run_bass_kernel_spmd(nc, [{"in_" + k: v for k, v in a.items()}], core_ids=[0])
    return r.results[0]["out_0"]
```

```python
import numpy as np
import concourse.bass as bass
from concourse import mybir
from contextlib import ExitStack

F32 = mybir.dt.float32
F16 = mybir.dt.float16
ALU = mybir.AluOpType
ACT = mybir.ActivationFunctionType
AX = mybir.AxisListType.X

B, S, D = 16, 256, 128
P = 128
T = S // P
CB = 2
CT, CS = CB * T, CB * S
CHUNKS = B // CB
FC = 4 * D // P
E0, HB = 8, 2
E1 = 4
H, HD = 16, 8
G, J = 4, 4
SLOT = P // J
U = 1 + E1
HALVES = G * T * 2
LEAD = 6
X_T, KV, R = 1, 2, 3
MIX, X1_OUT, X1_T = 5, 5, 7
FC_0, MLP, MLP_OUT = 8, 12, 13
Q_T, Q_OUT, K_T, K_OUT = 2, 4, 3, 3
OUT_T, NORMALISE, Y_T = 5, 6, 9
LOGITS = 9
PROJECT, PROJECT_OUT = 10, 10
SHIFT_T = 10
QKV, QKV_OUT = 12, 12
LOW_SUMS, HIGH_SUMS = 12, 2
HIGH = 0
RMS_EPS, LN_EPS = 1e-6, 1e-5
MASKED = -60000.0
DMA = 16

SHIFT_ROW, MASK_ROW = 3 * HD, 3 * HD + 1


class Unit:

    def __init__(self, sig, u, n, parity):
        self.s, self.u, self.n, self.parity = sig, u, n, parity


class LayerZeroSignals:

    def __init__(self, sem):
        self.ssq_ready = sem("ssq_ready")
        self.rstd_ready = sem("rstd_ready")
        self.xn_ready = sem("xn_ready")
        self.xT_ps = sem("xT_ps")
        self.xT_ready = sem("xT_ready")
        self.k_ps = sem("k_ps")
        self.k_sb_ready = sem("k_sb_ready")
        self.v_ps = sem("v_ps")
        self.r_ps = sem("r_ps")
        self.er_ready = sem("er_ready")
        self.kv_ready = sem("kv_ready")
        self.mixT_ready = sem("mixT_ready")
        self.mix_ps = sem("mix_ps")
        self.x1_ready = sem("x1_ready")
        self.fc_ps = sem("fc_ps")
        self.zhalf_ready = sem("zhalf_ready")
        self.h_ready = sem("h_ready")
        self.hfc_ready = sem("hfc_ready")
        self.mlp_ps = sem("mlp_ps")
        self.lnvar_ready = sem("lnvar_ready")
        self.logit_ps = sem("logit_ps")
        self.lg_ready = sem("lg_ready")
        self.pexp_ready = sem("pexp_ready")
        self.score_ready = sem("score_ready")
        self.scoreT_ps = sem("scoreT_ps")
        self.scoreT_ready = sem("scoreT_ready")
        self.acc0_ps = sem("acc0_ps")
        self.acc0_used = sem("acc0_used")
        self.acc_ready = sem("acc_ready")
        self.hmoe_ps = sem("hmoe_ps")
        self.hmoe_ready = sem("hmoe_ready")
        self.ymoe_ps = sem("ymoe_ps")
        self.ymoe_used = sem("ymoe_used")
        self.dve_step = sem("dve_step")
        self.pool_step = sem("pool_step")
        self.numbers = range(self.ssq_ready.num, self.pool_step.num + 1)


class GroupSignals:

    def __init__(self, sem):
        self.qkv_ps = sem("qkv_ps")
        self.qkv_ready = sem("qkv_ready")
        self.qkms_ready = sem("qkms_ready")
        self.rqk_ready = sem("rqk_ready")
        self.qn_ready = sem("qn_ready")
        self.v_ready = sem("v_ready")
        self.high_ready = sem("high_ready")
        self.q_split_ready = sem("q_split_ready")
        self.k_split_ready = sem("k_split_ready")
        self.tk_ps = sem("tk_ps")
        self.tq_ps = sem("tq_ps")
        self.kT_ready = sem("kT_ready")
        self.qT_ready = sem("qT_ready")
        self.diag01_ready = sem("diag01_ready")
        self.diag23_ready = sem("diag23_ready")
        self.row_cleared = sem("row_cleared")
        self.smax_ps = sem("smax_ps")
        self.smax_used = sem("smax_used")
        self.mneg_ready = sem("mneg_ready")
        self.mT_ps = sem("mT_ps")
        self.mT_ready = sem("mT_ready")
        self.shift_ready = sem("shift_ready")
        self.s_ps = sem("s_ps")
        self.probs_ready = sem("probs_ready")
        self.pv_done = sem("pv_done")
        self.oT_ready = sem("oT_ready")
        self.oN_ps = sem("oN_ps")
        self.yn_ready = sem("yn_ready")
        self.yT_ps = sem("yT_ps")
        self.yT_ready = sem("yT_ready")
        self.proj_ps = sem("proj_ps")
        self.proj_used = sem("proj_used")
        self.lnvar_ready = sem("lnvar_ready")
        self.rstd_ready = sem("rstd_ready")
        self.x5_ready = sem("x5_ready")
        self.x5T_ps = sem("x5T_ps")
        self.x5T_ready = sem("x5T_ready")
        self.logit_ps = sem("logit_ps")
        self.lg_ready = sem("lg_ready")
        self.pexp_ready = sem("pexp_ready")
        self.route_ready = sem("route_ready")
        self.scoreT_ps = sem("scoreT_ps")
        self.scoreT_ready = sem("scoreT_ready")
        self.acc0_ps = sem("acc0_ps")
        self.acc0_used = sem("acc0_used")
        self.x4_ready = sem("x4_ready")
        self.x4T_ps = sem("x4T_ps")
        self.x4T_ready = sem("x4T_ready")
        self.x4_used = sem("x4_used")
        self.y_ready = sem("y_ready")
        self.dve_step = sem("dve_step")
        self.pool_step = sem("pool_step")
        self.numbers = range(self.qkv_ps.num, self.pool_step.num + 1)


def program(nc, a, out):
    with ExitStack() as ctx:
        def sb(name, shape, dt=F32):
            return ctx.enter_context(nc.sbuf_tensor(name, shape, dt))

        def sem(name):
            return ctx.enter_context(nc.semaphore(name))

        wkvr = sb("wkvr", [D, 3, D])
        wo0 = sb("wo0", [D, D])
        wfc = sb("wfc", [D, FC * P])
        wmlp = sb("wmlp", [P, FC, D])
        wg = sb("wg", [D, E0])
        w1 = sb("w1", [D, E0, HB * P])
        b1 = sb("b1", [P, E0, HB])
        w2 = sb("w2", [P, E0, HB, D])
        b2 = sb("b2", [E0, D])
        wqkv = sb("wqkv", [D, U, 3 * D])
        bqkv = sb("bqkv", [P, U, 3 * D])
        wproj = sb("wproj", [D, U, D])
        bproj = sb("bproj", [P, D])
        bo = sb("bo", [E1, D])
        qk_w = sb("qk_w", [P, 2, HD])
        router_w = sb("router_w", [D, E1])
        router_b = sb("router_b", [P, E1])
        decay = sb("decay", [D, 2])
        mixer_scale = sb("mixer_scale", [P, D])
        mlp_scale = sb("mlp_scale", [P, D])
        ident = sb("ident", [P, P])
        ident16 = sb("ident16", [P, P], F16)
        half = sb("half", [P, 2 * T * H])
        prio = sb("prio", [P, E0])
        ew = sb("ew", [D, 2])
        ew_bc = sb("ew_bc", [D, S])

        x4_all = sb("x4_all", [P, B * T, D])

        ps = ctx.enter_context(nc.psum_tensor("ps", [P, 8, 512], F32))

        loaded = sem("loaded")
        const_ready = sem("const_ready")
        ew_ready = sem("ew_ready")
        diag_clear = sem("diag_clear")
        exp_decay = sem("exp_decay")
        x_loaded = sem("x_loaded")
        stored = sem("stored")
        batch_done = sem("batch_done")
        cleared = sem("cleared")
        passed = sem("passed")
        done = [sem(f"done{p}") for p in range(2)]
        clean = [sem(f"clean{p}") for p in range(2)]
        l0 = LayerZeroSignals(lambda name: sem(f"{name}_l0"))
        sets = [GroupSignals(lambda name, p=p: sem(f"{name}_g{p}")) for p in range(2)]

        loads = [
            (wkvr[:], a["wkvr"].rearrange("c i o -> i c o")), (wo0[:], a["wo0"]), (decay[:], a["decay"]),
            (mixer_scale[:], a["mixer_scale"].partition_broadcast(P)), (wfc[:], a["wfc"]),
            (wmlp[:], a["wmlp"].rearrange("(c p) d -> p c d", p=P)), (wg[:], a["wg"]),
            (mlp_scale[:], a["mlp_scale"].partition_broadcast(P)),
            (w1[:], a["w1"].rearrange("e i o -> i e o")), (b1[:], a["b1"].rearrange("e (c p) -> p e c", p=P)),
            (w2[:], a["w2"].rearrange("e (c p) d -> p e c d", p=P)), (b2[:], a["b2"]),
            (wqkv[:], a["wqkv"].rearrange("u i o -> i u o")), (bqkv[:], a["bqkv"].partition_broadcast(P)),
            (wproj[:], a["wproj"].rearrange("u i o -> i u o")), (bproj[:], a["bproj"].partition_broadcast(P)),
            (bo[:], a["bo"]), (qk_w[:], a["qk_w"].partition_broadcast(P)), (router_w[:], a["router_w"]),
            (router_b[:], a["router_b"].partition_broadcast(P)),
        ]
        CONSTS = 3

        def meet(eng):
            eng.drain().then_inc(batch_done, 1)
            eng.wait_ge(cleared, 1)
            eng.sem_inc(passed, 1)

        def meet_and_clear(pool):
            pool.drain().then_inc(batch_done, 1)
            pool.wait_ge(batch_done, 4)
            pool.sem_clear(l0.numbers)
            pool.sem_clear(batch_done)
            pool.sem_inc(cleared, 1)
            pool.wait_ge(passed, 3)
            pool.sem_clear(passed)
            pool.sem_clear(cleared)

        def tiles(x, t=T):
            return x.rearrange("p (t d) -> p t d", t=t)

        def softmax_top2(v, link, sig, src, n_e, n_t, bias, lg, pr, tk, oh1, oh2, st, exp_count):
            def bc(x):
                return x.unsqueeze(2).broadcast_to([P, n_t, n_e])

            pb = prio[:, 0:n_e].unsqueeze(1).broadcast_to([P, n_t, n_e])

            def before_exp():
                if bias is not None:
                    link(v.tensor_tensor(lg, src, bias[:].unsqueeze(1).broadcast_to([P, n_t, n_e]), ALU.add))
                else:
                    link(v.tensor_copy(lg, src))
                link(v.reduce_max(st[:, 0, :], lg, AX))
                v.tensor_tensor(lg, lg, bc(st[:, 0, :]), ALU.subtract).then_inc(sig.lg_ready, 1)

            def first_largest(src, top, one_hot):
                link(v.reduce_max(top, src, AX))
                link(v.tensor_tensor(tk, src, bc(top), ALU.is_equal))
                link(v.tensor_tensor(tk, tk, pb, ALU.mult))
                link(v.reduce_max(st[:, 5, :], tk, AX))
                link(v.tensor_tensor(one_hot, bc(st[:, 5, :]), pb, ALU.is_equal))

            def after_exp():
                v.wait_ge(sig.pexp_ready, exp_count)
                link(v.reduce_sum(st[:, 1, :], pr, AX))
                link(v.reciprocal(st[:, 2, :], st[:, 1, :]))
                link(v.tensor_tensor(pr, pr, bc(st[:, 2, :]), ALU.mult))
                first_largest(pr, st[:, 3, :], oh1)
                link(v.scalar_tensor_tensor(lg, oh1, -2.0, pr, ALU.mult, ALU.add))

            def second():
                first_largest(lg, st[:, 4, :], oh2)
                link(v.tensor_tensor(oh1, oh1, oh2, ALU.add))

            return before_exp, after_exp, second

        with nc.Block() as block:
            @block.sync
            def _(sp):
                for dst, src in loads:
                    sp.dma_start(dst, src, allow_slow_non_contiguous=True).then_inc(loaded, DMA)

            @block.gpsimd
            def _(pool):
                pool.memset(ident[:], 0.0).then_inc(const_ready, 1)
                pool.memset(half[:], -0.5)
                for e in range(E0):
                    last = pool.memset(prio[:, e:e + 1], float(E0 - e))
                last.then_inc(const_ready, 1)
                pool.wait_ge(const_ready, 1)
                pool.affine_select(out=ident[:], in_=ident[:], compare_op=ALU.not_equal, fill=1.0, base=0,
                                   pattern=[[-1, P]], channel_multiplier=1).then_inc(const_ready, 1)
                pool.wait_ge(const_ready, CONSTS)

            @block.scalar
            def _(act):
                act.wait_ge(loaded, DMA * len(loads))
                act.activation(ew[:, 0:1], decay[:, 0:1], ACT.Exp).then_inc(exp_decay, 1)
                act.wait_ge(exp_decay, 1)
                act.activation(decay[:, 0:1], ew[:, 0:1], ACT.Exp, scale=-1.0).then_inc(exp_decay, 1)
                act.activation(ew[:, 1:2], decay[:, 1:2], ACT.Exp).then_inc(exp_decay, 1)

            @block.vector
            def _(v):
                v.wait_ge(const_ready, CONSTS)
                v.tensor_copy(ident16[:], ident[:]).then_inc(ew_ready, 1)
                v.wait_ge(exp_decay, 3)
                v.tensor_scalar(ew_bc[:], decay[:, 0:1].broadcast_to([D, S]), 1.0, None,
                                ALU.mult).then_inc(ew_ready, 1)

            @block.tensor
            def _(pe):
                pe.wait_ge(loaded, DMA * len(loads))
                pe.wait_ge(ew_ready, 2)

        with ExitStack() as ph:
            def sb1(name, shape, dt=F32):
                return ph.enter_context(nc.sbuf_tensor(name, shape, dt))

            x_all = sb1("x_all", [P, B * T, D])
            junk = sb1("junk", [P, 2, CT, D])
            ssq = sb1("ssq", [P, 2, CT])
            var = sb1("var", [P, 4, CT])
            rstd = sb1("rstd", [P, 4, CT])
            bn6 = sb1("bn6", [P, 2, CT, 6])
            mv = sb1("mv", [P, 2, CT, 2])
            xn = sb1("xn", [P, CT, D])
            xT = sb1("xT", [D, CS])
            x3T = sb1("x3T", [D, CS])
            k_sb = sb1("k_sb", [D, CS])
            er = sb1("er", [D, CS])
            gate = sb1("gate", [D, CS])
            kv = sb1("kv", [D, CS])
            wkv = sb1("wkv", [D, CS])
            state = sb1("state", [D, CB, S + 1])
            mixT = sb1("mixT", [D, CS])
            tmp = sb1("tmp", [P, CT, D])
            x1 = sb1("x1", [P, CT, D])
            z_half = sb1("z_half", [P, FC, CS])
            h_fc = sb1("h_fc", [P, FC, CS])
            x3 = sb1("x3", [P, 2, CT, D])
            acc = sb1("acc", [P, CT, D])
            h_moe = sb1("h_moe", [P, 2, HB, CS])
            lg = sb1("lg", [P, CT, E0])
            pr = sb1("pr", [P, CT, E0])
            oh1 = sb1("oh1", [P, CT, E0])
            oh2 = sb1("oh2", [P, CT, E0])
            tk = sb1("tk", [P, CT, E0])
            st = sb1("st", [P, 8, CT])
            score = sb1("score", [P, CT, E0])
            scoreT = sb1("scoreT", [E0, CS])
            h_bank = [ps[:, 0:2, :], ps[:, 2:4, :]]
            y_bank = [ps[:, 4, :], ps[:, 5, :]]
            ma, mb = ps[:, 6, :], ps[:, 7, :]
            s = l0
            block = ph.enter_context(nc.Block())

            def chunk(x, c, t=None):
                return x[:, bass.ds(c * CT, CT), :] if t is None else x[:, bass.ds(c * CT + t, 1), :].rearrange("p a d -> p (a d)")

            def over_chunks(eng, experts, ahead, sync):
                for i in range(2 * E0):
                    ahead(i, 0)
                sync(eng)
                with eng.Fori(0, CHUNKS - 1) as c:
                    for i in range(2 * E0):
                        experts(i, c)
                        ahead(i, c + 1)
                    experts(2 * E0, c)
                    sync(eng)
                for i in range(2 * E0 + 1):
                    experts(i, CHUNKS - 1)

            @block.sync
            def _(sp):
                for c in range(2):
                    lo, hi = (0, CT) if c == 0 else (CT, B * T)
                    sp.dma_start(x_all[:, lo:hi, :], a["x"].rearrange("b (t p) d -> p (b t) d", p=P)[:, lo:hi, :])\
                      .then_inc(x_loaded, DMA)

            @block.gpsimd
            def _(pool):
                steps = [0]

                def inverse_root(k, src, scale, eps):
                    steps[0] += 1
                    pool.tensor_scalar(var[:, k, :], src, scale, eps, ALU.mult, ALU.add).then_inc(s.pool_step, 1)
                    pool.wait_ge(s.pool_step, steps[0])
                    pool.tensor_tensor(rstd[:, k, :], var[:, k, :], half[:, 0:CT], ALU.pow).then_inc(s.rstd_ready, 1)

                def ahead(i, c):
                    if i == 0:
                        pool.wait_ge(s.ssq_ready, 1)
                        inverse_root(0, ssq[:, 0, :], 1.0 / D, RMS_EPS)
                    if i == X1_OUT + 1:
                        pool.wait_ge(s.ssq_ready, 2)
                        inverse_root(1, ssq[:, 1, :], 1.0 / D, RMS_EPS)
                    if i == MLP_OUT:
                        pool.wait_ge(s.lnvar_ready, 1)
                        inverse_root(2, mv[:, 0, :, 1], 1.0, LN_EPS)

                def experts(i, c):
                    if i == 2 * E0:
                        pool.wait_ge(s.acc_ready, 1)
                        inverse_root(3, mv[:, 1, :, 1], 1.0, LN_EPS)

                def sync(eng):
                    meet_and_clear(eng)
                    steps[0] = 0

                pool.memset(state[:, :, 0:1], 0.0)
                over_chunks(pool, experts, ahead, sync)

            @block.scalar
            def _(act):
                act.wait_ge(x_loaded, 2 * DMA)

                def ahead(i, c):
                    if i == 0:
                        for t in range(CT):
                            last = act.activation(junk[:, 0, t, :], chunk(x_all, c, t), ACT.Square,
                                                  accum_out=ssq[:, 0, t:t + 1])
                        last.then_inc(s.ssq_ready, 1)
                    if i == X_T:
                        act.wait_ge(s.xT_ps, 1)
                        act.copy(xT[:], ma).then_inc(s.xT_ready, 1)
                    if i == KV:
                        act.wait_ge(s.k_ps, 1)
                        act.copy(k_sb[:], ma).then_inc(s.k_sb_ready, 1)
                    if i == R:
                        act.wait_ge(s.r_ps, 1)
                        act.activation(er[:], ma, ACT.Exp, scale=-1.0).then_inc(s.er_ready, 1)
                    if i == X1_OUT + 1:
                        act.wait_ge(s.x1_ready, 1)
                        for t in range(CT):
                            last = act.activation(junk[:, 1, t, :], x1[:, t, :], ACT.Square, accum_out=ssq[:, 1, t:t + 1])
                        last.then_inc(s.ssq_ready, 1)
                    if i == X1_T:
                        act.wait_ge(s.xT_ps, 2)
                        act.copy(xT[:], ma).then_inc(s.xT_ready, 1)
                    if FC_0 <= i < FC_0 + FC:
                        f = i - FC_0
                        act.wait_ge(s.fc_ps, f + 1)
                        act.activation(z_half[:, f, :], (mb, ma)[f % 2], ACT.Copy, scale=0.5).then_inc(s.zhalf_ready, 1)
                    if i == 15:
                        act.wait_ge(s.xT_ps, 3)
                        act.copy(x3T[:], mb).then_inc(s.xT_ready, 1)

                def experts(i, c):
                    if i == 1:
                        act.wait_ge(s.lg_ready, 1)
                        act.activation(pr[:], lg[:], ACT.Exp).then_inc(s.pexp_ready, 1)
                    if i % 2 == 0 and i < 2 * E0:
                        e = i // 2
                        act.wait_ge(s.hmoe_ps, e + 1)
                        for k in range(HB):
                            last = act.activation(h_moe[:, e % 2, k, :], h_bank[e % 2][:, k, :], ACT.Relu,
                                                  bias=b1[:, e, k:k + 1])
                        last.then_inc(s.hmoe_ready, 1)
                    if i == 5:
                        act.wait_ge(s.scoreT_ps, 1)
                        act.copy(scoreT[:], mb[0:E0, :]).then_inc(s.scoreT_ready, 1)

                over_chunks(act, experts, ahead, meet)

            @block.vector
            def _(v):
                v.wait_ge(x_loaded, 2 * DMA)
                steps = [0]

                def link(ins):
                    steps[0] += 1
                    ins.then_inc(s.dve_step, 1)
                    v.wait_ge(s.dve_step, steps[0])

                def bn(k, src):
                    for t in range(CT):
                        last = v.bn_stats(bn6[:, k, t, :], src[:, t, :])
                    link(last)
                    for t in range(CT):
                        last = v.bn_aggr(mv[:, k, t, :], bn6[:, k, t, :])
                    return last

                def apply(k, src, dst):
                    for t in range(CT):
                        last = v.tensor_scalar(dst(t), src[:, t, :], mv[:, k, t, 0:1], rstd[:, 2 + k, t:t + 1],
                                               ALU.subtract, ALU.mult)
                    return last

                def ahead(i, c):
                    if i == 0:
                        v.wait_ge(s.rstd_ready, 1)
                        for t in range(CT):
                            last = v.tensor_scalar(xn[:, t, :], chunk(x_all, c, t), rstd[:, 0, t:t + 1], None, ALU.mult)
                        last.then_inc(s.xn_ready, 1)
                    if i == KV:
                        v.wait_ge(s.k_sb_ready, 1)
                        v.wait_ge(s.v_ps, 1)
                        v.tensor_tensor(kv[:], k_sb[:], mb, ALU.mult).then_inc(s.kv_ready, 1)
                        v.wait_ge(s.kv_ready, 1)
                        for n in range(CB):
                            last = v.tensor_tensor_scan(state[:, n, 1:S + 1], ew_bc[:], kv[:, n * S:(n + 1) * S], 0.0,
                                                        ALU.mult, ALU.add)
                        link(last)
                    if i == R:
                        link(v.scalar_tensor_tensor(wkv[:].rearrange("p (n s) -> p n s", n=CB),
                                                    kv[:].rearrange("p (n s) -> p n s", n=CB), ew[:, 1:2],
                                                    state[:, :, 0:S], ALU.mult, ALU.add))
                        v.wait_ge(s.er_ready, 1)
                        link(v.tensor_scalar(gate[:], er[:], 1.0, None, ALU.add))
                        link(v.reciprocal(gate[:], gate[:]))
                        v.tensor_tensor(mixT[:], wkv[:], gate[:], ALU.mult).then_inc(s.mixT_ready, 1)
                    if i == X1_OUT:
                        v.wait_ge(s.mix_ps, 1)
                        msc = mixer_scale[:].unsqueeze(1).broadcast_to([P, CT, D])
                        link(v.tensor_tensor(tmp[:], tiles(ma, CT), msc, ALU.mult))
                        v.tensor_tensor(x1[:], tmp[:], chunk(x_all, c), ALU.add).then_inc(s.x1_ready, 1)
                    if i == X1_OUT + 1:
                        v.wait_ge(s.rstd_ready, 2)
                        for t in range(CT):
                            last = v.tensor_scalar(xn[:, t, :], x1[:, t, :], rstd[:, 1, t:t + 1], None, ALU.mult)
                        last.then_inc(s.xn_ready, 1)
                    if FC_0 <= i < FC_0 + FC:
                        f = i - FC_0
                        v.wait_ge(s.zhalf_ready, f + 1)
                        v.tensor_tensor(h_fc[:, f, :], z_half[:, f, :], (mb, ma)[f % 2], ALU.max).then_inc(s.h_ready, 1)
                        v.wait_ge(s.h_ready, f + 1)
                        v.tensor_tensor(h_fc[:, f, :], h_fc[:, f, :], h_fc[:, f, :], ALU.mult).then_inc(s.hfc_ready, 1)
                    if i == MLP_OUT:
                        v.wait_ge(s.mlp_ps, 1)
                        lsc = mlp_scale[:].unsqueeze(1).broadcast_to([P, CT, D])
                        link(v.tensor_tensor(tmp[:], tiles(ma, CT), lsc, ALU.mult))
                        link(v.tensor_tensor(tmp[:], tmp[:], x1[:], ALU.add))
                        link(v.tensor_tensor(tmp[:], tmp[:], chunk(x_all, c), ALU.add))
                        bn(0, tmp).then_inc(s.lnvar_ready, 1)
                        v.wait_ge(s.rstd_ready, 3)
                        apply(0, tmp, lambda t: x3[:, 0, t, :]).then_inc(s.xn_ready, 1)

                parts = softmax_top2(v, link, s, ma.rearrange("p (t x) -> p t x", t=CT)[:, :, 0:E0], E0, CT, None,
                                     lg[:], pr[:], tk[:], oh1[:], oh2[:], st, 1)

                def experts(i, c):
                    if i == 0:
                        link(v.tensor_copy(x3[:, 1], x3[:, 0]))
                        v.wait_ge(s.logit_ps, 1)
                        parts[0]()
                    if i == 1:
                        parts[1]()
                        parts[2]()
                        link(v.tensor_tensor(score[:], oh1[:], pr[:], ALU.mult))
                        link(v.reduce_sum(st[:, 6, :], score[:], AX))
                        link(v.reciprocal(st[:, 7, :], st[:, 6, :]))
                        v.tensor_tensor(score[:], score[:], st[:, 7, :].unsqueeze(2).broadcast_to([P, CT, E0]),
                                        ALU.mult).then_inc(s.score_ready, 1)
                        v.wait_ge(s.score_ready, 1)
                    if i >= 3 and i % 2 == 1 or i == 2 * E0:
                        for e in ([0] if i == 3 else [(i - 3) // 2] if i < 2 * E0 else [E0 - 1]):
                            v.wait_ge(s.ymoe_ps, e + 1)
                            for t in range(CT):
                                last = v.scalar_tensor_tensor(acc[:, t, :], y_bank[e % 2][:, t * D:(t + 1) * D],
                                                              score[:, t, e:e + 1], (x3[:, 1] if e == 0 else acc)[:, t, :],
                                                              ALU.mult, ALU.add)
                            last.then_inc(s.ymoe_used, 1)
                            v.wait_ge(s.ymoe_used, e + 1)
                    if i == 7:
                        v.wait_ge(s.acc0_ps, 1)
                        v.tensor_tensor(acc[:], acc[:], tiles(mb, CT), ALU.add).then_inc(s.acc0_used, 1)
                        v.wait_ge(s.acc0_used, 1)
                    if i == 2 * E0:
                        bn(1, acc).then_inc(s.acc_ready, 1)
                        v.wait_ge(s.rstd_ready, 4 if ahead_too[0] else 1)
                        link(apply(1, acc, lambda t: chunk(x4_all, c, t)))

                def sync(eng):
                    meet(eng)
                    steps[0] = 0

                ahead_too = [True]

                def last_too(i, c):
                    ahead_too[0] = not isinstance(c, int)
                    experts(i, c)

                over_chunks(v, last_too, ahead, sync)

            @block.tensor
            def _(pe):
                def mm(o, l, r, start=True, stop=True):
                    return pe.matmul(o, l, r, start=start, stop=stop)

                def transposes(dst, src):
                    for t in range(CT):
                        last = pe.transpose(dst[:, t * P:(t + 1) * P], src[:, t, :], ident[:])
                    return last

                def ahead(i, c):
                    if i == X_T:
                        pe.wait_ge(s.xn_ready, 1)
                        transposes(ma, xn).then_inc(s.xT_ps, 1)
                    if i == KV:
                        pe.wait_ge(s.xT_ready, 1)
                        mm(ma, wkvr[:, 0, :], xT[:]).then_inc(s.k_ps, 1)
                        mm(mb, wkvr[:, 1, :], xT[:]).then_inc(s.v_ps, 1)
                    if i == R:
                        pe.wait_ge(s.k_sb_ready, 1)
                        mm(ma, wkvr[:, 2, :], xT[:]).then_inc(s.r_ps, 1)
                    if i == MIX:
                        pe.wait_ge(s.mixT_ready, 1)
                        for t in range(CT):
                            last = mm(ma[:, t * D:(t + 1) * D], mixT[:, t * P:(t + 1) * P], wo0[:])
                        last.then_inc(s.mix_ps, 1)
                    if i == X1_T:
                        pe.wait_ge(s.xn_ready, 2)
                        transposes(ma, xn).then_inc(s.xT_ps, 1)
                    if FC_0 <= i < FC_0 + FC:
                        f = i - FC_0
                        if f == 0:
                            pe.wait_ge(s.xT_ready, 2)
                            if not isinstance(c, int):
                                pe.wait_ge(s.acc0_used, 1)
                        if f >= 2:
                            pe.wait_ge(s.h_ready, f - 1)
                        mm((mb, ma)[f % 2], wfc[:, f * P:(f + 1) * P], xT[:]).then_inc(s.fc_ps, 1)
                    if i == MLP:
                        pe.wait_ge(s.hfc_ready, FC)
                        for t in range(CT):
                            for f in range(FC):
                                last = mm(ma[:, t * D:(t + 1) * D], h_fc[:, f, t * P:(t + 1) * P], wmlp[:, f, :],
                                          start=f == 0, stop=f == FC - 1)
                        last.then_inc(s.mlp_ps, 1)
                    if i == 15:
                        pe.wait_ge(s.xn_ready, 3)
                        transposes(mb, x3[:, 0]).then_inc(s.xT_ps, 1)

                def experts(i, c):
                    if i == 0:
                        for t in range(CT):
                            last = mm(ma[:, t * P:t * P + E0], x3T[:, t * P:(t + 1) * P], wg[:])
                        last.then_inc(s.logit_ps, 1)
                        hidden(0)
                        pe.wait_ge(s.lg_ready, 1)
                    if i % 2 == 0 and i // 2 + 1 < E0:
                        hidden(i // 2 + 1)
                    if i == 4:
                        pe.wait_ge(s.score_ready, 1)
                        if not isinstance(c, int):
                            pe.wait_ge(s.kv_ready, 1)
                        for t in range(CT):
                            last = pe.transpose(mb[0:E0, t * P:(t + 1) * P], score[:, t, :], ident[:])
                        last.then_inc(s.scoreT_ps, 1)
                    if i == 6:
                        pe.wait_ge(s.scoreT_ready, 1)
                        for t in range(CT):
                            last = mm(mb[:, t * D:(t + 1) * D], scoreT[:, t * P:(t + 1) * P], b2[:])
                        last.then_inc(s.acc0_ps, 1)
                    if i % 2 == 1:
                        e = i // 2
                        pe.wait_ge(s.hmoe_ready, e + 1)
                        if e >= 2:
                            pe.wait_ge(s.ymoe_used, e - 1)
                        for t in range(CT):
                            for k in range(HB):
                                last = mm(y_bank[e % 2][:, t * D:(t + 1) * D], h_moe[:, e % 2, k, t * P:(t + 1) * P],
                                          w2[:, e, k, :], start=k == 0, stop=k == HB - 1)
                        last.then_inc(s.ymoe_ps, 1)

                def hidden(e):
                    if e >= 2:
                        pe.wait_ge(s.hmoe_ready, e - 1)
                    for k in range(HB):
                        last = mm(h_bank[e % 2][:, k, :], w1[:, e, k * P:(k + 1) * P], x3T[:])
                    last.then_inc(s.hmoe_ps, 1)

                over_chunks(pe, experts, ahead, meet)

        def unit(group, u):
            return Unit(sets[group % 2], u, u if group < B - 1 else u - 1, group % 2)

        def norms_of(unit):
            return 1 if unit.u == 0 or unit.n < unit.u else 2

        def units(group):
            return [unit(group, u) if (u == 0 and group < B - 1) or (u > 0 and group >= 0) else None for u in range(U)]

        def over_units(eng, period):
            def group(g, n, chain):
                seq = [units(g - 1)[-1]] + units(g) + (units(g + 1) if g + 1 < B else [None] * U)
                for p in range(U):
                    period(p, g, n, chain, seq[p:p + 5])

            for p in (2, 3, 4):
                seq = [None] * (U + 1) + units(-1)
                period(p, -2, -2, 0, seq[p:p + 5])
            group(-1, -1, 1)
            group(0, 0, 0)
            with eng.Fori(0, (B - 4) // 2) as r:
                group(1, r * 2 + 1, 1)
                group(2, r * 2 + 2, 0)
            for g in range(B - 3, B):
                group(g, g, g % 2)
            period(0, B, B, 0, [unit(B - 1, U - 1), None, None, None, None])

        with ExitStack() as ph:
            def sb2(name, shape, dt=F32):
                return ph.enter_context(nc.sbuf_tensor(name, shape, dt))

            x4 = sb2("x4", [P, T, D])
            x4T = sb2("x4T", [D, S])
            x5 = sb2("x5", [P, T, D])
            x5T = sb2("x5T", [D, S])
            x5_sum = sb2("x5_sum", [P, T, D])
            acc = sb2("acc2", [P, 2, T, D])
            y = sb2("y", [P, 2, T, D])
            bn6 = sb2("bn6_2", [P, T, 6])
            mv = sb2("mv_2", [P, 2, T, 2])
            var = sb2("var_2", [P, 2, T])
            rstd = sb2("rstd_2", [P, 2, T])
            lg = sb2("lg_2", [P, T, E1])
            pr = sb2("pr_2", [P, T, E1])
            oh1 = sb2("oh1_2", [P, T, E1])
            oh2 = sb2("oh2_2", [P, T, E1])
            tk = sb2("tk_2", [P, T, E1])
            st = sb2("st_2", [P, 8, T])
            key_mask = sb2("key_mask", [P, 2, T, E1])
            w_tok = sb2("w_tok", [P, 2, T, E1])
            scoreT = sb2("scoreT_2", [E1, S])
            qkv = sb2("qkv", [P, 3, T, D])
            sq = sb2("sq", [P, 2, T, D])
            ms = sb2("ms", [P, 2 * T * H])
            rqk = sb2("rqk", [P, 2 * T * H])
            q_split = sb2("q_split", [P, T, H, SLOT], F16)
            k_split = sb2("k_split", [P, T, H, SLOT], F16)
            v_ext = sb2("v_ext", [P, U, T, H, SLOT])
            qT = sb2("qT", [P, G, S], F16)
            kT = sb2("kT", [P, U, G, S], F16)
            q_diag = sb2("q_diag", [P, U, J, G, S], F16)
            zero_row = sb2("zero_row", [1, J * G * S], F16)
            mx = sb2("mx", [P, U, T, H])
            mneg = sb2("mneg", [P, U, T, H], F16)
            mT = sb2("mT", [H, U, S], F16)
            PB = 4
            probs = sb2("probs", [P, PB, J, S])
            oT = sb2("oT", [P, G, S])
            rden = sb2("rden", [P, T * H])
            y_n = sb2("y_n", [P, T, D])
            yT = sb2("yT", [D, S])

            def s_bank(i):
                return ps[:, i % 2, :]

            def max_bank(i):
                return ps[:, 2 + i % 2, :]

            def o_bank(i):
                return ps[:, 4 + i, :]

            m0, m1 = ps[:, 6, :], ps[:, 7, :]
            both = ps[:, 6:8, :]
            rden_t = rden[:].rearrange("p (b t h) -> p b t h", b=2, t=T)

            with nc.Block() as block:
                @block.gpsimd
                def _(pool):
                    for x in (q_split, k_split, zero_row):
                        pool.memset(x[:].bitcast(F32), 0.0).then_inc(const_ready, 1)
                    pool.memset(v_ext[:], 0.0).then_inc(const_ready, 1)
                    pool.wait_ge(const_ready, CONSTS + 4)
                    pool.memset(q_split[:, :, :, MASK_ROW:MASK_ROW + 1], 1.0)
                    for h in range(0, H, J):
                        pool.memset(k_split[:, :, h:h + 1, SHIFT_ROW:SHIFT_ROW + 1], 1.0)
                    for u in range(U):
                        last = pool.memset(v_ext[:, u, :, :, HD:HD + 1], 1.0)
                    last.then_inc(const_ready, 1)
                    pool.wait_ge(const_ready, CONSTS + 5)

                @block.vector
                def _(v):
                    v.memset(q_diag[:].bitcast(F32), 0.0).then_inc(diag_clear, 1)
                    v.wait_ge(diag_clear, 1)

            block = ph.enter_context(nc.Block())

            def hand_back(eng, p, g):
                if p == 1 and g >= -1:
                    eng.drain().then_inc(done[(g - 1) % 2], 1)

            def await_clean(eng, p, g):
                if p == 2 and g >= -1:
                    eng.wait_ge(clean[(g + 1) % 2], 1)
                    eng.drain()

            def half_of(i, nxt, nxt2):
                return (nxt, i + LEAD) if i + LEAD < HALVES else (nxt2, i + LEAD - HALVES)

            @block.sync
            def _(sp):
                def period(p, g, n, chain, k):
                    prev, cur, nxt, nxt2, nxt3 = k
                    hand_back(sp, p, g)
                    if prev:
                        sp.wait_ge(prev.s.probs_ready, (prev.n + 1) * HALVES)
                        sp.dma_start(q_diag[SHIFT_ROW:SHIFT_ROW + 1, prev.u], zero_row[:]).then_inc(prev.s.row_cleared, DMA)
                    if nxt2:
                        sp.wait_ge(nxt2.s.qT_ready, nxt2.n + 1)
                        for j in range(J):
                            sp.dma_start(q_diag[SLOT * j:SLOT * (j + 1), nxt2.u, j, :, :], qT[SLOT * j:SLOT * (j + 1), :, :])\
                              .then_inc((nxt2.s.diag01_ready, nxt2.s.diag23_ready)[j // 2], DMA)
                    if nxt:
                        sp.wait_ge(nxt.s.mT_ready, nxt.n + 1)
                        sp.dma_start(q_diag[SHIFT_ROW:SHIFT_ROW + 1, nxt.u], mT[:, nxt.u, :]).then_inc(nxt.s.shift_ready, DMA)
                    if prev:
                        sp.wait_ge(prev.s.row_cleared, (prev.n + 1) * DMA)
                    await_clean(sp, p, g)
                    if prev and p == 0:
                        sp.wait_ge(prev.s.y_ready, 1)
                        sp.dma_start(out[bass.ds(n - 1, 1), :, :].rearrange("b (t p) d -> p (b t) d", p=P),
                                     y[:, prev.parity]).then_inc(stored, DMA)

                over_units(sp, period)
                sp.wait_ge(stored, DMA * B)

            @block.gpsimd
            def _(pool):
                steps = {0: 0, 1: 0}

                def link(ins, chain):
                    steps[chain] += 1
                    ins.then_inc(sets[chain].pool_step, 1)
                    pool.wait_ge(sets[chain].pool_step, steps[chain])

                def part(x, c):
                    return x[:].rearrange("p t h s -> p (t h) s")[:, :, c * HD:(c + 1) * HD]

                def low_parts(unit):
                    if unit.u == 0:
                        pool.memset(k_split[:, :, :, MASK_ROW:MASK_ROW + 1], 0.0)
                    else:
                        for t in range(T):
                            pool.tensor_copy(k_split[:, t, :, MASK_ROW:MASK_ROW + 1],
                                             key_mask[:, unit.parity, t, unit.u - 1:unit.u].unsqueeze(1).broadcast_to([P, H, 1]))
                    pool.wait_ge(unit.s.high_ready, 2 * unit.n + 1)
                    pool.tensor_tensor(part(q_split, 2), qkv[:, 0].rearrange("p t (h d) -> p (t h) d", h=H),
                                       part(q_split, 0), ALU.subtract).then_inc(unit.s.q_split_ready, 1)
                    pool.wait_ge(unit.s.high_ready, 2 * unit.n + 2)
                    pool.tensor_tensor(part(k_split, 1), qkv[:, 1].rearrange("p t (h d) -> p (t h) d", h=H),
                                       part(k_split, 0), ALU.subtract).then_inc(unit.s.k_split_ready, 1)

                def inverse_root(unit, k):
                    link(pool.tensor_scalar(var[:, k, :], mv[:, k, :, 1], 1.0, LN_EPS, ALU.mult, ALU.add), unit.parity)
                    pool.tensor_tensor(rstd[:, k, :], var[:, k, :], half[:, 0:T], ALU.pow).then_inc(unit.s.rstd_ready, 1)

                def period(p, g, n, chain, k):
                    prev, cur, nxt, nxt2, nxt3 = k
                    hand_back(pool, p, g)
                    if p == 2 and g >= -1:
                        q = (g - 1) % 2
                        pool.wait_ge(done[q], 5)
                        pool.sem_clear(sets[q].numbers)
                        pool.sem_clear(done[q])
                        pool.sem_clear(clean[1 - q])
                        pool.sem_inc(clean[q], 1)
                        steps[q] = 0
                        await_clean(pool, p, g)
                    if nxt2 and nxt2.u == 0:
                        low_parts(nxt2)
                    if prev and prev.u in (0, U - 1):
                        pool.wait_ge(prev.s.lnvar_ready, norms_of(prev))
                        inverse_root(prev, 0 if prev.u == 0 else 1)
                    if p == (1 if g >= -1 else 2) and g + 1 < B - 1:
                        if g >= -1:
                            pool.wait_ge(sets[g % 2].x4_used, 1)
                        pool.tensor_copy(x4[:], x4_all[:, bass.ds((n + 2) * T, T), :]).then_inc(sets[g % 2].x4_ready, 1)
                    if nxt3:
                        pool.wait_ge(nxt3.s.qkv_ready, nxt3.n + 1)
                        pool.tensor_copy(v_ext[:, nxt3.u, :, :, 0:HD],
                                         qkv[:, 2].rearrange("p t (h d) -> p t h d", h=H)).then_inc(nxt3.s.v_ready, 1)
                        if nxt3.u == 0:
                            pool.wait_ge(nxt3.s.qkms_ready, 1)
                            link(pool.tensor_scalar(ms[:], ms[:], 1.0 / HD, RMS_EPS, ALU.mult, ALU.add), nxt3.parity)
                            pool.tensor_tensor(rqk[:], ms[:], half[:], ALU.pow).then_inc(nxt3.s.rqk_ready, 1)
                        else:
                            if nxt3.u == 1:
                                pool.wait_ge(sets[1 - nxt3.parity].route_ready, 1)
                            low_parts(nxt3)

                over_units(pool, period)

            @block.scalar
            def _(act):
                def high_parts(unit, src, dst, places):
                    x = qkv[:, src].rearrange("p t (h d) -> p (t h) d", h=H)
                    for place in places:
                        last = act.copy(dst[:].rearrange("p t h s -> p (t h) s")[:, :, place * HD:(place + 1) * HD], x)
                    last.then_inc(unit.s.high_ready, 1)

                def period(p, g, n, chain, k):
                    prev, cur, nxt, nxt2, nxt3 = k
                    hand_back(act, p, g)
                    for i in range(HALVES):
                        if cur:
                            act.wait_ge(cur.s.s_ps, cur.n * HALVES + i + 1)
                            act.activation(probs[:, (i // 2) % PB, 2 * (i % 2):2 * (i % 2) + 2, :].rearrange("p j s -> p (j s)"),
                                           s_bank(i), ACT.Exp, scale=HD ** -0.5 if cur.u == 0 else 0.5)\
                               .then_inc(cur.s.probs_ready, 1)
                        if i == 1 and p == 2 and -1 <= g < B - 1:
                            act.wait_ge(sets[g % 2].x5T_ps, 1)
                            act.copy(x5T[:], m0[:, 0:S]).then_inc(sets[g % 2].x5T_ready, 1)
                        if i == 1 and p == 2 and nxt3:
                            act.wait_ge(sets[g % 2].x4T_ps, 1)
                            act.copy(x4T[:], m0[:, S:2 * S]).then_inc(sets[g % 2].x4T_ready, 1)
                        if i == 1 and p == 3 and g >= -1 and g < B - 1:
                            act.wait_ge(sets[g % 2].scoreT_ps, 1)
                            act.copy(scoreT[:], m0[0:E1, 0:S]).then_inc(sets[g % 2].scoreT_ready, 1)
                        if i == HIGH and nxt2:
                            if nxt2.u == 0:
                                act.wait_ge(nxt2.s.qn_ready, 1)
                            else:
                                act.wait_ge(nxt2.s.qkv_ready, nxt2.n + 1)
                            high_parts(nxt2, 0, q_split, (0, 1))
                        if i == HIGH + 1 and nxt2:
                            high_parts(nxt2, 1, k_split, (0, 2))
                        if i == HIGH_SUMS and prev:
                            act.wait_ge(prev.s.pv_done, prev.n * (HALVES // 2) + HALVES // 2)
                            act.copy(oT[:, 2:4, :].rearrange("p g s -> p (g s)"), o_bank(1)).then_inc(prev.s.oT_ready, 1)
                        if i == Y_T and prev:
                            act.wait_ge(prev.s.yT_ps, prev.n + 1)
                            act.copy(yT[:], m0[:, 0:S]).then_inc(prev.s.yT_ready, 1)
                        if i == Q_OUT and nxt2:
                            act.wait_ge(nxt2.s.tq_ps, nxt2.n + 1)
                            act.copy(qT[:, 0:2].rearrange("p g s -> p (g s)"), m1.bitcast(F16)[:, 0:2 * S])
                        if i == Q_OUT + 1 and nxt2:
                            act.copy(qT[:, 2:4].rearrange("p g s -> p (g s)"), m1.bitcast(F16)[:, 2 * S:4 * S])\
                               .then_inc(nxt2.s.qT_ready, 1)
                        if i == LOGITS + 2 and p == 2 and g >= -1 and g < B - 1:
                            act.wait_ge(sets[g % 2].lg_ready, 1)
                            act.activation(pr[:], lg[:], ACT.Exp).then_inc(sets[g % 2].pexp_ready, 1)
                        if i == LOW_SUMS and cur:
                            act.wait_ge(cur.s.pv_done, cur.n * (HALVES // 2) + HALVES // 4)
                            act.copy(oT[:, 0:2, :].rearrange("p g s -> p (g s)"), o_bank(0)).then_inc(cur.s.oT_ready, 1)
                        if i == SHIFT_T:
                            await_clean(act, p, g)
                        if i == SHIFT_T + 1 and nxt:
                            act.wait_ge(nxt.s.mT_ps, nxt.n + 1)
                            act.copy(mT[:, nxt.u], m0.bitcast(F16)[0:H, 0:S]).then_inc(nxt.s.mT_ready, 1)

                over_units(act, period)

            @block.vector
            def _(v):
                steps = {0: 0, 1: 0}
                now = [0]

                def link(ins):
                    chain = now[0]
                    steps[chain] += 1
                    ins.then_inc(sets[chain].dve_step, 1)
                    v.wait_ge(sets[chain].dve_step, steps[chain])

                def layer_norm(unit, k, src, dst, dst_sem):
                    for t in range(T):
                        last = v.bn_stats(bn6[:, t, :], src[:, t, :])
                    link(last)
                    for t in range(T):
                        last = v.bn_aggr(mv[:, k, t, :], bn6[:, t, :])
                    last.then_inc(unit.s.lnvar_ready, 1)
                    yield
                    v.wait_ge(unit.s.rstd_ready, norms_of(unit))
                    for t in range(T):
                        last = v.tensor_scalar(dst[:, t, :], src[:, t, :], mv[:, k, t, 0:1], rstd[:, k, t:t + 1],
                                               ALU.subtract, ALU.mult)
                    last.then_inc(dst_sem, 1)
                    yield

                def period(p, g, n, chain, k):
                    prev, cur, nxt, nxt2, nxt3 = k
                    if p == 0:
                        steps[chain] = 0
                    now[0] = chain
                    hand_back(v, p, g)
                    own = sets[g % 2]
                    routing = p in (2, 3) and -1 <= g < B - 1
                    if routing:
                        parts = softmax_top2(v, link, own, m1.rearrange("p (t x) -> p t x", t=T)[:, :, 0:E1], E1, T,
                                             router_b, lg[:], pr[:], tk[:], oh1[:], oh2[:], st, 1)
                    if nxt2 and nxt2.u == 0:
                        v.wait_ge(nxt2.s.rqk_ready, 1)
                        qk = qkv[:, 0:2].rearrange("p c t (h d) -> p (c t h) d", h=H)
                        link(v.tensor_tensor(qk, qk, rqk[:].unsqueeze(2).broadcast_to([P, 2 * T * H, HD]), ALU.mult))
                        for c in range(2):
                            qc = qkv[:, c].rearrange("p t (h d) -> p (t h) d", h=H)
                            last = v.tensor_tensor(qc, qc, qk_w[:, c, :].unsqueeze(1).broadcast_to([P, T * H, HD]), ALU.mult)
                        last.then_inc(nxt2.s.qn_ready, 1)
                    for i in range(HALVES):
                        unit, m = half_of(i, nxt, nxt2)
                        if unit:
                            t, g_, jp = m // (2 * G), m // 2 % G, m % 2
                            v.wait_ge(unit.s.smax_ps, unit.n * HALVES + m + 1)
                            v.reduce_max(mx[:, unit.u, t, J * g_ + 2 * jp:J * g_ + 2 * jp + 2],
                                         max_bank(m).rearrange("p (c k) -> p c k", c=2), AX).then_inc(unit.s.smax_used, 1)
                        if i == HALVES - 1 - LEAD and nxt:
                            v.wait_ge(nxt.s.smax_used, (nxt.n + 1) * HALVES)
                            v.tensor_scalar(mneg[:, nxt.u].rearrange("p t (j g) -> p t g j", j=J),
                                            mx[:, nxt.u].rearrange("p t (g j) -> p t g j", j=J), -1.0, None,
                                            ALU.mult).then_inc(nxt.s.mneg_ready, 1)
                        if i == NORMALISE and prev:
                            v.wait_ge(prev.s.oN_ps, 2 * prev.n + 2)
                            link(v.reciprocal(rden[:], both.rearrange("p b (x s) -> p (b x) s", s=SLOT)[:, :, HD]))
                            if prev.u > 0:
                                link(v.tensor_tensor(rden_t, rden_t, w_tok[:, prev.parity, :, prev.u - 1].unsqueeze(1)
                                                     .unsqueeze(3).broadcast_to([P, 2, T, H // 2]), ALU.mult))
                        if i == NORMALISE + 1 and prev:
                            for b in range(2):
                                last = v.tensor_tensor(
                                    y_n[:, :, b * (D // 2):(b + 1) * (D // 2)].rearrange("p t (h d) -> p t h d", h=H // 2),
                                    both[:, b, :].rearrange("p (t h s) -> p t h s", t=T, s=SLOT)[:, :, :, 0:HD],
                                    rden_t[:, b].unsqueeze(3).broadcast_to([P, T, H // 2, HD]), ALU.mult)
                            last.then_inc(prev.s.yn_ready, 1)
                        if i == LOGITS and routing and p == 2:
                            v.wait_ge(own.logit_ps, 1)
                            parts[0]()
                        if i == LOGITS and p == 3 and routing:
                            v.wait_ge(own.acc0_ps, 1)
                            v.tensor_tensor(acc[:, 1 - g % 2], tiles(m1[:, 0:T * D]), x5[:], ALU.add).then_inc(own.acc0_used, 1)
                        if i == K_OUT and nxt2:
                            v.wait_ge(nxt2.s.tk_ps, nxt2.n + 1)
                            v.tensor_copy(kT[:, nxt2.u, 0:2].rearrange("p g s -> p (g s)"), m0.bitcast(F16)[:, 0:2 * S])
                        if i == K_OUT + 1 and nxt2:
                            v.tensor_copy(kT[:, nxt2.u, 2:4].rearrange("p g s -> p (g s)"), m0.bitcast(F16)[:, 2 * S:4 * S])\
                             .then_inc(nxt2.s.kT_ready, 1)
                        if i == LOGITS + 3 and routing and p == 2:
                            parts[1]()
                        if i == LOGITS + 4 and routing and p == 2:
                            parts[2]()
                            link(v.tensor_scalar(key_mask[:, 1 - g % 2], oh1[:], -MASKED, MASKED, ALU.mult, ALU.add))
                            v.tensor_tensor(w_tok[:, 1 - g % 2], oh1[:], pr[:], ALU.mult).then_inc(own.route_ready, 1)
                        if i == PROJECT_OUT and prev:
                            v.wait_ge(prev.s.proj_ps, prev.n + 1)
                            pj = tiles(m1[:, 0:T * D])
                            if prev.u == 0:
                                v.tensor_tensor(x5_sum[:], pj, bproj[:].unsqueeze(1).broadcast_to([P, T, D]),
                                                ALU.add).then_inc(prev.s.proj_used, 1)
                                v.wait_ge(prev.s.proj_used, prev.n + 1)
                                v.tensor_tensor(x5_sum[:], x5_sum[:], x4[:], ALU.add).then_inc(prev.s.x4_used, 1)
                                v.wait_ge(prev.s.x4_used, 1)
                                norm = layer_norm(prev, 0, x5_sum, x5, prev.s.x5_ready)
                            else:
                                a_ = acc[:, prev.parity]
                                v.tensor_tensor(a_, a_, pj, ALU.add).then_inc(prev.s.proj_used, 1)
                                if prev.u == U - 1:
                                    v.wait_ge(prev.s.proj_used, prev.n + 1)
                                    norm = layer_norm(prev, 1, a_, y[:, prev.parity], prev.s.y_ready)
                            if prev.u in (0, U - 1):
                                next(norm)
                        if i == 13 and prev and prev.u in (0, U - 1):
                            next(norm)
                        if i == 13:
                            await_clean(v, p, g)
                        if i in (QKV_OUT, QKV_OUT + 1) and nxt3:
                            t = QKV_OUT + 1 - i
                            v.wait_ge(nxt3.s.qkv_ps, T * nxt3.n + T - t)
                            last = v.tensor_tensor(qkv[:, :, t, :], both[:, t, 0:3 * D].rearrange("p (c d) -> p c d", c=3),
                                                   bqkv[:, nxt3.u, :].rearrange("p (c d) -> p c d", c=3), ALU.add)
                        if i == QKV_OUT + 1 and nxt3:
                            last.then_inc(nxt3.s.qkv_ready, 1)
                            if nxt3.u == 0:
                                v.wait_ge(nxt3.s.qkv_ready, 1)
                                link(v.tensor_tensor(sq[:], qkv[:, 0:2], qkv[:, 0:2], ALU.mult))
                                v.reduce_sum(ms[:], sq[:].rearrange("p c t (h d) -> p (c t h) d", h=H), AX)\
                                 .then_inc(nxt3.s.qkms_ready, 1)

                over_units(v, period)

            @block.tensor
            def _(pe):
                def mm(o, l, r, start=True, stop=True):
                    return pe.matmul(o, l, r, start=start, stop=stop)

                def scores(unit, i, before):
                    g, t, jp = i // 4, i // 2 % T, i % 2
                    if i == 0:
                        pe.wait_ge(unit.s.shift_ready, (unit.n + 1) * DMA)
                    if i >= 2:
                        pe.wait_ge(unit.s.probs_ready, unit.n * HALVES + i - 1)
                    elif before:
                        pe.wait_ge(before.s.probs_ready, before.n * HALVES + HALVES - 1 + i)
                    mm(s_bank(i), kT[:, unit.u, g, t * P:(t + 1) * P], q_diag[:, unit.u, 2 * jp:2 * jp + 2, g, :])\
                        .then_inc(unit.s.s_ps, 1)

                def weigh(unit, i):
                    g, t = i // T, i % T
                    pe.wait_ge(unit.s.probs_ready, unit.n * HALVES + 2 * i + 2)
                    if i == 0:
                        pe.wait_ge(unit.s.v_ready, unit.n + 1)
                    for j in range(J):
                        last = mm(o_bank(g // 2)[SLOT * j:SLOT * (j + 1), (g % 2) * S:(g % 2 + 1) * S],
                                  v_ext[:, unit.u, t, J * g + j, :], probs[:, i % PB, j, :], start=t == 0, stop=t == T - 1)
                    last.then_inc(unit.s.pv_done, 1)

                def max_scores(unit, m, before):
                    t, g, jp = m // (2 * G), m // 2 % G, m % 2
                    if m == 0:
                        pe.wait_ge(unit.s.diag01_ready, (unit.n + 1) * (2 * DMA))
                        pe.wait_ge(unit.s.kT_ready, unit.n + 1)
                    if m == 1:
                        pe.wait_ge(unit.s.diag23_ready, (unit.n + 1) * (2 * DMA))
                    if m >= 2:
                        pe.wait_ge(unit.s.smax_used, unit.n * HALVES + m - 1)
                    elif before:
                        pe.wait_ge(before.s.smax_used, before.n * HALVES + HALVES - 1 + m)
                    for j in range(2):
                        last = mm(max_bank(m)[:, j * S:(j + 1) * S], q_diag[:, unit.u, 2 * jp + j, g, t * P:(t + 1) * P],
                                  kT[:, unit.u, g, :])
                    last.then_inc(unit.s.smax_ps, 1)

                def turn(unit, dst, src, written, ready):
                    pe.wait_ge(written, unit.n + 1)
                    for g in range(G):
                        for t in range(T):
                            last = pe.transpose(dst.bitcast(F16)[:, g * S + t * P:g * S + (t + 1) * P],
                                                src[:, t, J * g:J * (g + 1), :].rearrange("p h s -> p (h s)"), ident16[:])
                    last.then_inc(ready, 1)

                def period(p, g, n, chain, k):
                    prev, cur, nxt, nxt2, nxt3 = k
                    own = sets[g % 2]
                    hand_back(pe, p, g)
                    routing = -1 <= g < B - 1
                    for i in range(HALVES):
                        unit, m = half_of(i, nxt, nxt2)
                        if unit:
                            max_scores(unit, m, nxt if unit is nxt2 else None)
                        if i + 1 < HALVES and cur:
                            scores(cur, i + 1, prev)
                        if i == 1 and prev:
                            weigh(prev, HALVES // 2 - 1)
                        if i >= 3 and i % 2 == 1 and cur:
                            if i in (3, 11) and prev:
                                pe.wait_ge(prev.s.oT_ready, 2 * prev.n + (1 if i == 3 else 2))
                            weigh(cur, (i - 3) // 2)
                        if i == 1 and p == 2 and nxt3:
                            if nxt2:
                                pe.wait_ge(nxt2.s.qkv_ready, nxt2.n + 1)
                            pe.wait_ge(own.x4_ready, 1)
                            for t in range(T):
                                last = pe.transpose(m0[:, S + t * P:S + (t + 1) * P], x4[:, t, :], ident[:])
                            last.then_inc(own.x4T_ps, 1)
                        if i == 1 and p in (2, 3) and routing:
                            if nxt2:
                                pe.wait_ge(nxt2.s.qkv_ready, nxt2.n + 1)
                            if p == 2:
                                pe.wait_ge(own.x5_ready, 1)
                                for t in range(T):
                                    last = pe.transpose(m0[:, t * P:(t + 1) * P], x5[:, t, :], ident[:])
                                last.then_inc(own.x5T_ps, 1)
                            else:
                                pe.wait_ge(own.route_ready, 1)
                                for t in range(T):
                                    last = pe.transpose(m0[0:E1, t * P:(t + 1) * P], w_tok[:, 1 - g % 2, t, :], ident[:])
                                last.then_inc(own.scoreT_ps, 1)
                        if i == Q_T and nxt2:
                            turn(nxt2, m1, q_split, nxt2.s.q_split_ready, nxt2.s.tq_ps)
                        if i == K_T:
                            if p == 2 and nxt3:
                                pe.wait_ge(own.x4T_ready, 1)
                            if p == 2 and routing:
                                pe.wait_ge(own.x5T_ready, 1)
                            if p == 3 and routing:
                                pe.wait_ge(own.scoreT_ready, 1)
                            if nxt2:
                                turn(nxt2, m0, k_split, nxt2.s.k_split_ready, nxt2.s.tk_ps)
                        if i == OUT_T and nxt2:
                            pe.wait_ge(nxt2.s.kT_ready, nxt2.n + 1)
                        if i == OUT_T + 1 and nxt2:
                            pe.wait_ge(nxt2.s.qT_ready, nxt2.n + 1)
                        if i in (OUT_T, OUT_T + 1) and prev:
                            b = i - OUT_T
                            pe.wait_ge(prev.s.oT_ready, 2 * prev.n + b + 1)
                            for t in range(T):
                                for g_ in range(2):
                                    last = pe.transpose(both[:, b, (2 * t + g_) * P:(2 * t + g_ + 1) * P],
                                                        oT[:, 2 * b + g_, t * P:(t + 1) * P], ident[:])
                            last.then_inc(prev.s.oN_ps, 1)
                        if i == Y_T and prev:
                            pe.wait_ge(prev.s.yn_ready, prev.n + 1)
                            for t in range(T):
                                last = pe.transpose(m0[:, t * P:(t + 1) * P], y_n[:, t, :], ident[:])
                            last.then_inc(prev.s.yT_ps, 1)
                        if i == LOGITS and routing and prev:
                            pe.wait_ge(prev.s.yn_ready, prev.n + 1)
                        if i == LOGITS and routing and p == 2:
                            for t in range(T):
                                last = mm(m1[:, t * S:t * S + E1], x5T[:, t * P:(t + 1) * P], router_w[:])
                            last.then_inc(own.logit_ps, 1)
                        if i == LOGITS and routing and p == 3:
                            for t in range(T):
                                last = mm(m1[:, t * D:(t + 1) * D], scoreT[:, t * P:(t + 1) * P], bo[:])
                            last.then_inc(own.acc0_ps, 1)
                        if i == PROJECT:
                            if p == 2 and routing:
                                pe.wait_ge(own.lg_ready, 1)
                            if p == 3 and routing:
                                pe.wait_ge(own.acc0_used, 1)
                            if prev:
                                pe.wait_ge(prev.s.yT_ready, prev.n + 1)
                                for t in range(T):
                                    last = mm(m1[:, t * D:(t + 1) * D], yT[:, t * P:(t + 1) * P], wproj[:, prev.u, :])
                                last.then_inc(prev.s.proj_ps, 1)
                        if i == SHIFT_T:
                            await_clean(pe, p, g)
                            if prev:
                                pe.wait_ge(prev.s.yT_ready, prev.n + 1)
                            if nxt:
                                pe.wait_ge(nxt.s.mneg_ready, nxt.n + 1)
                                for t in range(T):
                                    last = pe.transpose(m0.bitcast(F16)[0:H, t * P:(t + 1) * P], mneg[:, nxt.u, t, :], ident16[:])
                                last.then_inc(nxt.s.mT_ps, 1)
                        if i == QKV and prev:
                            pe.wait_ge(prev.s.proj_used, prev.n + 1)
                        if i == QKV + 1 and nxt:
                            pe.wait_ge(nxt.s.mT_ready, nxt.n + 1)
                        if i in (QKV, QKV + 1) and nxt3:
                            t = QKV + 1 - i
                            src = x4T if nxt3.u == 0 else x5T
                            mm(both[:, t, 0:3 * D], src[:, t * P:(t + 1) * P], wqkv[:, nxt3.u, :]).then_inc(nxt3.s.qkv_ps, 1)
                        if i == HALVES - 1 and nxt:
                            scores(nxt, 0, cur)

                over_units(pe, period)


def kernel(**inputs):
    import concourse.bacc as bacc
    from concourse.bass_utils import run_bass_kernel_spmd

    f = {k: np.ascontiguousarray(v) for k, v in inputs.items()}
    c = np.ascontiguousarray
    a = {
        "x": f["L0_attn_x"],
        "wkvr": c(np.stack([f["L0_attn_Wk"].T, f["L0_attn_Wv"].T, f["L0_attn_Wr"].T])),
        "wo0": c(f["L0_attn_Wo"].T),
        "decay": c(np.stack([f["L0_attn_time_decay"], f["L0_attn_time_first"]], axis=1)),
        "mixer_scale": f["L0_attn_mixer_scale"],
        "wfc": c(f["L0_attn_Wfc"].T),
        "wmlp": c(f["L0_attn_Wmlp"].T),
        "mlp_scale": f["L0_attn_mlp_scale"],
        "wg": f["L0_ffn_Wg"], "w1": f["L0_ffn_W1"], "b1": f["L0_ffn_b1"], "w2": f["L0_ffn_W2"], "b2": f["L0_ffn_b2"],
        "wqkv": c(np.concatenate([f["L1_attn_W_qkv"][None],
                                  np.concatenate([f["L1_ffn_wq"], f["L1_ffn_wk"], f["L1_ffn_wv"]], axis=2)])),
        "bqkv": c(np.concatenate([f["L1_attn_b_qkv"][None],
                                  np.concatenate([f["L1_ffn_bq"], f["L1_ffn_bk"], f["L1_ffn_bv"]], axis=1)])),
        "wproj": c(np.concatenate([f["L1_attn_W_proj"][None], f["L1_ffn_wo"]])),
        "bproj": f["L1_attn_b_proj"],
        "bo": f["L1_ffn_bo"],
        "qk_w": c(np.stack([f["L1_attn_qn_w"], f["L1_attn_kn_w"]])),
        "router_w": f["L1_ffn_router_w"], "router_b": f["L1_ffn_router_b"],
    }
    nc = bacc.Bacc("TRN2", target_bir_lowering=False, num_devices=1)
    aps = {k: nc.dram_tensor("in_" + k, v.shape, F32, kind="ExternalInput").ap() for k, v in a.items()}
    out = nc.dram_tensor("out_0", (B, S, D), F32, kind="ExternalOutput").ap()
    program(nc, aps, out)
    r = run_bass_kernel_spmd(nc, [{"in_" + k: v for k, v in a.items()}], core_ids=[0])
    return r.results[0]["out_0"]
```
